# Optimizing a Trainium2 kernel written in Bass

```python
import numpy as np
import jax
import jax.numpy as jnp

def _softmax(x, axis=-1):
    return jax.nn.softmax(x, axis=axis)

def _gelu(x):
    return jax.nn.gelu(x, approximate=True)

def _silu(x):
    return jax.nn.silu(x)

def _sigmoid(x):
    return jax.nn.sigmoid(x)

def _layernorm(x, axis=-1, eps=1e-05):
    m = jnp.mean(x, axis=axis, keepdims=True)
    v = jnp.var(x, axis=axis, keepdims=True)
    return (x - m) / jnp.sqrt(v + eps)

def _scatter_add(tgt, idx, src, axis=0):
    return tgt.at[idx].add(src)

def _segment_sum(src, seg, n):
    return jax.ops.segment_sum(src, seg, n)
kernel_name = 'mk_early_fusion_d1_tok_img1024_r4_3b089a'

def setup_inputs(seed: int=0):
    np.random.seed(seed)
    _w = jnp.asarray

    def _rec_inputs():
        import jax
        import jax.numpy as jnp
        _rk = jax.random.key(seed)
        x = -0.000222058 + 0.999998 * jax.random.normal(jax.random.fold_in(_rk, 1), (8, 3, 112, 112), jnp.float32)
        txt = 0.000402619 + 0.577528 * jax.random.normal(jax.random.fold_in(_rk, 2), (8, 128, 256), jnp.float32)
        return (x, txt)
    x, txt = _rec_inputs()

    def _L0_tok_setup():
        import jax, jax.numpy as jnp
        import numpy as np
        P = 16
        key = jax.random.key(seed)
        kx, kw, kb = jax.random.split(key, 3)
        B, C, H, W_ = (32, 3, 128, 128)
        in_dim, embed_dim = (C * P * P, 256)
        x = jax.random.normal(kx, (B, C, H, W_), dtype=jnp.float32)
        bound = 1.0 / np.sqrt(in_dim)
        W = jax.random.uniform(kw, (embed_dim, in_dim), minval=-bound, maxval=bound, dtype=jnp.float32)
        b = jax.random.uniform(kb, (embed_dim,), minval=-bound, maxval=bound, dtype=jnp.float32)
        return {'x': x, 'W': W, 'b': b}
    _L0_tok_all = _L0_tok_setup()
    _L0_tok_in = {k: v for k, v in _L0_tok_all.items() if k in ('W', 'b')}
    del _L0_tok_all

    def _L0_attn_setup():
        import jax, jax.numpy as jnp
        import numpy as np
        B, N, D = (2, 512, 256)
        H, M = (8, 64)
        DK = D // H
        EPS = 1e-05

        def _gsa(q, k, v, s, g):
            b = q.shape[1]

            def step1(hk, t):
                q_t, k_t, s_t, g_t = t
                hk = hk * jnp.exp(g_t)[:, :, None, :] + k_t[..., :, None] * s_t[..., None, :]
                ok = jnp.einsum('bhk,bhkm->bhm', q_t, hk)
                return (hk, ok)
            hk0 = jnp.zeros((b, H, DK, M), q.dtype)
            _, ok = jax.lax.scan(step1, hk0, (q, k, s, g))
            qv = jax.nn.softmax(ok, axis=-1)

            def step2(hv, t):
                qv_t, s_t, v_t, g_t = t
                hv = hv * jnp.exp(g_t)[..., :, None] + s_t[..., :, None] * v_t[..., None, :]
                ov = jnp.einsum('bhm,bhmv->bhv', qv_t, hv)
                return (hv, ov)
            hv0 = jnp.zeros((b, H, M, DK), q.dtype)
            _, ov = jax.lax.scan(step2, hv0, (qv, s, v, g))
            return ov
        key = jax.random.key(seed)
        ks = jax.random.split(key, 9)
        std = 0.02
        return {'x': jax.random.normal(ks[0], (B, N, D), jnp.float32), 'Wq': jax.random.normal(ks[1], (D, D), jnp.float32) * std, 'Wk': jax.random.normal(ks[2], (D, D), jnp.float32) * std, 'Wv': jax.random.normal(ks[3], (D, D), jnp.float32) * std, 'Wf1': jax.random.normal(ks[4], (D, DK), jnp.float32) * std, 'Wf2': jax.random.normal(ks[5], (DK, H * M), jnp.float32) * std, 'Wg1': jax.random.normal(ks[6], (D, DK), jnp.float32) * std, 'Wg2': jax.random.normal(ks[7], (DK, D), jnp.float32) * std, 'Wo': jax.random.normal(ks[8], (D, D), jnp.float32) * std, 'norm_w': jnp.ones((D,), jnp.float32)}
    _L0_attn_all = _L0_attn_setup()
    _L0_attn_in = {k: v for k, v in _L0_attn_all.items() if k in ('Wq', 'Wk', 'Wv', 'Wf1', 'Wf2', 'Wg1', 'Wg2', 'Wo', 'norm_w')}
    del _L0_attn_all

    def _L0_ffn_setup():
        import math
        import jax, jax.numpy as jnp
        import numpy as np
        B, S, D, F, E = (8, 512, 256, 1024, 8)
        CAPACITY_FACTOR = 1.0
        key = jax.random.key(seed)
        k1, k2, k3, k4 = jax.random.split(key, 4)
        x = jax.random.normal(k1, (B, S, D), dtype=jnp.float32)
        Wr = jax.random.normal(k2, (D, E), dtype=jnp.float32) * (1.0 / math.sqrt(D))
        W1 = jax.random.normal(k3, (E, D, F), dtype=jnp.float32) * (1.0 / math.sqrt(D))
        W2 = jax.random.normal(k4, (E, F, D), dtype=jnp.float32) * (1.0 / math.sqrt(F))
        return {'x': x, 'Wr': Wr, 'W1': W1, 'W2': W2}
    _L0_ffn_all = _L0_ffn_setup()
    _L0_ffn_in = {k: v for k, v in _L0_ffn_all.items() if k in ('Wr', 'W1', 'W2')}
    del _L0_ffn_all
    return {'x': x, 'txt': txt, 'L0_tok_W': _L0_tok_in['W'], 'L0_tok_b': _L0_tok_in['b'], 'L0_attn_Wq': _L0_attn_in['Wq'], 'L0_attn_Wk': _L0_attn_in['Wk'], 'L0_attn_Wv': _L0_attn_in['Wv'], 'L0_attn_Wf1': _L0_attn_in['Wf1'], 'L0_attn_Wf2': _L0_attn_in['Wf2'], 'L0_attn_Wg1': _L0_attn_in['Wg1'], 'L0_attn_Wg2': _L0_attn_in['Wg2'], 'L0_attn_Wo': _L0_attn_in['Wo'], 'L0_attn_norm_w': _L0_attn_in['norm_w'], 'L0_ffn_Wr': _L0_ffn_in['Wr'], 'L0_ffn_W1': _L0_ffn_in['W1'], 'L0_ffn_W2': _L0_ffn_in['W2']}

def reference(x, txt, L0_tok_W, L0_tok_b, L0_attn_Wq, L0_attn_Wk, L0_attn_Wv, L0_attn_Wf1, L0_attn_Wf2, L0_attn_Wg1, L0_attn_Wg2, L0_attn_Wo, L0_attn_norm_w, L0_ffn_Wr, L0_ffn_W1, L0_ffn_W2):
    import jax
    import jax.numpy as jnp

    def _L0_tok_ref(x, W, b):
        import jax, jax.numpy as jnp
        import numpy as np
        P = 16
        B, C, H, Wd = x.shape
        h, w = (H // P, Wd // P)
        patches = x.reshape(B, C, h, P, w, P).transpose(0, 2, 4, 1, 3, 5)
        patches = patches.reshape(B, h * w, C * P * P)
        return jnp.einsum('bld,ed->ble', patches, W) + b

    def _L0_attn_ref(x, Wq, Wk, Wv, Wf1, Wf2, Wg1, Wg2, Wo, norm_w):
        import jax, jax.numpy as jnp
        import numpy as np
        B, N, D = (2, 512, 256)
        H, M = (8, 64)
        DK = D // H
        EPS = 1e-05

        def _gsa(q, k, v, s, g):
            b = q.shape[1]

            def step1(hk, t):
                q_t, k_t, s_t, g_t = t
                hk = hk * jnp.exp(g_t)[:, :, None, :] + k_t[..., :, None] * s_t[..., None, :]
                ok = jnp.einsum('bhk,bhkm->bhm', q_t, hk)
                return (hk, ok)
            hk0 = jnp.zeros((b, H, DK, M), q.dtype)
            _, ok = jax.lax.scan(step1, hk0, (q, k, s, g))
            qv = jax.nn.softmax(ok, axis=-1)

            def step2(hv, t):
                qv_t, s_t, v_t, g_t = t
                hv = hv * jnp.exp(g_t)[..., :, None] + s_t[..., :, None] * v_t[..., None, :]
                ov = jnp.einsum('bhm,bhmv->bhv', qv_t, hv)
                return (hv, ov)
            hv0 = jnp.zeros((b, H, M, DK), q.dtype)
            _, ov = jax.lax.scan(step2, hv0, (qv, s, v, g))
            return ov
        b, n, d = x.shape
        q = jax.nn.silu(x @ Wq).reshape(b, n, H, DK)
        k = jax.nn.silu(x @ Wk).reshape(b, n, H, DK)
        v = (x @ Wv).reshape(b, n, H, DK)
        f = x @ Wf1 @ Wf2
        log_f = jax.nn.log_sigmoid(f).reshape(b, n, H, M)
        s = 1.0 - jnp.exp(log_f)
        tm = lambda a: jnp.swapaxes(a, 0, 1)
        ov = _gsa(tm(q), tm(k), tm(v), tm(s), tm(log_f))
        out = tm(ov).reshape(b, n, d)
        gate = x @ Wg1 @ Wg2
        out = out * jax.nn.sigmoid(gate)
        og = out.reshape(b, n, H, DK)
        og = og * jax.lax.rsqrt(jnp.mean(og * og, axis=-1, keepdims=True) + EPS)
        out = og.reshape(b, n, d) * norm_w
        return out @ Wo

    def _L0_ffn_ref(x, Wr, W1, W2):
        import math
        import jax, jax.numpy as jnp
        import numpy as np
        B, S, D, F, E = (8, 512, 256, 1024, 8)
        CAPACITY_FACTOR = 1.0
        b, s, d = x.shape
        t = b * s
        cap = max(math.ceil(t * CAPACITY_FACTOR / E), 1)
        xf = x.reshape(t, d)
        probs = jax.nn.softmax(xf.astype(jnp.float32) @ Wr, axis=-1)
        eidx = jnp.argmax(probs, axis=-1)
        p_tok = jnp.take_along_axis(probs, eidx[:, None], axis=1)[:, 0]
        onehot = jax.nn.one_hot(eidx, E, dtype=jnp.int32)
        rank_all = jnp.cumsum(onehot, axis=0) - onehot
        rank = jnp.take_along_axis(rank_all, eidx[:, None], axis=1)[:, 0]
        keep = rank < cap
        slot = jnp.where(keep, rank, cap)
        dispatch = jnp.zeros((E, cap + 1), dtype=jnp.int32).at[eidx, slot].set(jnp.arange(t, dtype=jnp.int32))
        valid = jnp.zeros((E, cap + 1), dtype=bool).at[eidx, slot].set(keep)
        dispatch = dispatch[:, :cap]
        valid = valid[:, :cap]
        xe = xf[dispatch]
        h = jnp.maximum(jnp.einsum('ecd,edf->ecf', xe, W1), 0.0)
        ye = jnp.einsum('ecf,efd->ecd', h, W2)
        pe = p_tok[dispatch]
        ye = ye * (pe * valid.astype(ye.dtype))[:, :, None]
        y = jnp.zeros((t, d), dtype=x.dtype).at[dispatch.reshape(-1)].add(ye.reshape(E * cap, d).astype(x.dtype))
        return y.reshape(b, s, d)
    h = _L0_tok_ref(x, L0_tok_W, L0_tok_b)
    h = jnp.concatenate([h, txt], axis=1)
    h = h + _L0_attn_ref(_layernorm(h, axis=-1), L0_attn_Wq, L0_attn_Wk, L0_attn_Wv, L0_attn_Wf1, L0_attn_Wf2, L0_attn_Wg1, L0_attn_Wg2, L0_attn_Wo, L0_attn_norm_w)
    h = h + _L0_ffn_ref(_layernorm(h, axis=-1), L0_ffn_Wr, L0_ffn_W1, L0_ffn_W2)
    return h

_drawn_inputs = setup_inputs


def setup_inputs(seed=0):
    import zlib

    import numpy as np

    out = dict(_drawn_inputs(seed))
    spreads = {'L0_attn_norm_w': (1.0, 0.2)}
    factors = {'L0_attn_Wq': 8.0, 'L0_attn_Wk': 8.0, 'L0_attn_Wf1': 3.816, 'L0_attn_Wf2': 5.909}
    for name, (base, spread) in spreads.items():
        noise = np.random.default_rng([zlib.crc32(name.encode()), seed]).standard_normal(out[name].shape)
        drawn = base * np.exp(spread * noise) if base else spread * noise
        out[name] = jnp.asarray(drawn.astype(out[name].dtype))
    for name, factor in factors.items():
        out[name] = (out[name] * factor).astype(out[name].dtype)
    return out
```

```python
from contextlib import ExitStack

import numpy as np
import concourse.bass as bass
from concourse import mybir

ALU = mybir.AluOpType
ACT = mybir.ActivationFunctionType
F32 = mybir.dt.float32
U32 = mybir.dt.uint32
AX_X = mybir.AxisListType.X

P = 128
B = 8
IMG = 49
TXT = 128
N = IMG + TXT
R = (N + 1) // 2
PATCH = 16
PD = 3 * PATCH * PATCH
KP = PD // P
D = 256
KD = D // P
H, M, DK = 8, 64, 32
HM = H * M
F = 1024
KF = F // P
E = 8
CAP = B * N // E
SLOTS = 2 * R
MID = R // 2
CUT = 64
LN_EPS = 1e-5
RMS_EPS = 1e-5
FAR = 8192.0
ZC = 8
COLS = D + 4
C_NMR, C_RSTD, C_TOK, C_PROB = D, D + 1, D + 2, D + 3
ABIG = 1e30

CONST = {}
_at = 0
for _name, _w in (("ident", P), ("mask", 3 * R), ("centre", R), ("cross0", R), ("cross1", R), ("before", R),
                  ("ones", R), ("rev", 2 * E), ("ebase", 2 * E), ("valid", 2), ("far", 2), ("tok", 2),
                  ("neghalf", 2), ("lneps", 2), ("validE", 2 * E)):
    CONST[_name] = (_at, _at + _w)
    _at += _w
CONST_COLS = _at

PAIRED = "patch_in text_in table_io h1_stored out_rows w1_in w2_in rows_in".split()
SEMS = """const_in wts_in bias_in table_clear zero_set rows_stored rows_dispatched
 emb_ps h_img stats1 mv1 ve1 rstd1 xn xnT_ps xnT fg_ps fgT qk_ps f_ps v_ps g_ps
 q_abs q_exp q_ln q_lsg q_sig qkT f_abs f_exp f_ln logf f_sig s g_abs g_exp g_ln g_lsg g_sig v
 d_ps e_ps eD ekD ecD S_rows ST_ps ST
 pa_ps pa pb_ps pb o_ps u umax umx pexp Z rZ QE QET_ps QET aa_ps aa ab_ps ab ov_ps ogn sq ss ss2 ss3 ss4 ss5 og
 rz2 ogT_ps ogT wo_ps h1 stats2 mv2 ve2 rstd2 nmr xf xfT_ps xfT lg_ps lmax ldm lexp lsum prob pick pickmax oh
 ohv rank_ps over eslot slotx slotoh slotsum slot acc1 acc2 tokset toknext wo_scaled
 xe_rows xeT_ps xeT hid_ps hid go_dispatch go_scatter ye_ps yeT yb_ps yout idx0 idx""".split()


def program(nc, patches, txt, tok_w, tok_b, wq, wk, wv, wfg1, wf2, wg2, wo, norm_w, wr, w1, w2, consts, out):
    with ExitStack() as ctx:
        def sb(name, shape, dt=F32):
            return ctx.enter_context(nc.sbuf_tensor(name, shape, dt))

        sem = {n: ctx.enter_context(nc.semaphore(n)) for n in SEMS}
        sem.update({n: [ctx.enter_context(nc.semaphore(f"{n}{par}")) for par in range(2)] for n in PAIRED})
        psF = ctx.enter_context(nc.psum_tensor("psF", [P, 4, 512], F32))
        psB = ctx.enter_context(nc.psum_tensor("psB", [P, 4, 512], F32))
        table = nc.dram_tensor("table", [E * SLOTS, COLS], F32, kind="Internal").ap()

        cst = sb("cst", [P, CONST_COLS])
        tokw = sb("tokw", [P, KP, D])
        bias = sb("bias", [IMG, D])
        wqs, wks, wvs, wos = (sb(n, [P, KD, D]) for n in ("wqs", "wks", "wvs", "wos"))
        won = sb("won", [P, KD, D])
        nw = sb("nw", [P, KD])
        wfg = sb("wfg", [P, KD, 2 * DK])
        wf2s = sb("wf2s", [DK, HM])
        wg2s = sb("wg2s", [2 * DK, D])
        wrs = sb("wrs", [P, KD, E])
        xpat = sb("xpat", [P, 2, KP, IMG])
        h = sb("h", [R, 2, 2, D])
        st1 = sb("st1", [R, 2, 6]); mv1 = sb("mv1", [R, 2, 2]); ve1 = sb("ve1", [R, 2]); rs1 = sb("rs1", [R, 2])
        xn = sb("xn", [R, 2, D])
        xnT = sb("xnT", [P, KD, 2 * R])
        fgT = sb("fgT", [2 * DK, 2 * R])
        qab = sb("qab", [P, 2, 2 * KD * R]); qln = sb("qln", [P, 2, 2 * KD * R])
        qkT = sb("qkT", [P, 2, 2, KD, 2 * R])
        fab = sb("fab", [R, 2, HM]); logf = sb("logf", [R, 2, HM])
        sig = sb("sig", [R, 2, HM]); srow = sb("srow", [R, 2, HM])
        gab = sb("gab", [R, 2 * D]); sg = sb("sg", [R, 2, 2 * D])
        v = sb("v", [R, 2, 2, D])
        eD = sb("eD", [R, 2, 2, HM]); ek = sb("ek", [R, 3, HM])
        S = sb("S", [R, 2, 3, HM])
        ST = sb("ST", [P, 2, 4, 3 * R])
        PT = sb("PT", [R, H, 3 * R]); AT = sb("AT", [R, H, 3 * R])
        u = sb("u", [R, 2, HM]); mx = sb("mx", [R, 2 * H])
        um = pexp = u
        Z = sb("Z", [R, 2 * H]); rZ = sb("rZ", [R, 2 * H])
        rz2 = sb("rz2", [R, 2 * H]); QE = sb("QE", [R, 2, HM]); QET = sb("QET", [P, 4, 2 * R])
        ogn = sb("ogn", [R, 2, D]); sq = sb("sq", [R, 2, D]); og = sb("og", [R, 2, D])
        ss = sb("ss", [R, 6, 2 * H]); halfH = sb("halfH", [R, 2 * H])
        ogT = sb("ogT", [P, KD, 2 * R])
        rows = sb("rows", [R, 2, 2, COLS])
        st2 = sb("st2", [R, 2, 6]); mv2 = sb("mv2", [R, 2, 2]); ve2 = sb("ve2", [R, 2])
        xf = sb("xf", [R, 2, D]); xfT = sb("xfT", [P, KD, 2 * R])
        rt = sb("rt", [R, 12, 2 * E]); rsm = sb("rsm", [R, 8, 2])
        oh = sb("oh", [R, 2, E]); acc = sb("acc", [R, E]); acct = sb("acct", [R, E]); tokc = sb("tokc", [R, 2])
        slot = sb("slot", [R, 2, 2], U32)
        zero = sb("zero", [R, 16 // ZC * COLS])
        w1s = sb("w1s", [P, 2, KD, F]); w2s = sb("w2s", [P, 2, KF, D])
        er = sb("er", [R, 2, 2, COLS]); xe = sb("xe", [R, 2, D]); xeT = sb("xeT", [P, KD, SLOTS])
        hid = sb("hid", [P, KF, SLOTS]); yeT = sb("yeT", [P, KD, SLOTS]); yo = sb("yo", [R, 2, 2, D])
        ix0 = sb("ix0", [R, 2]); ix = sb("ix", [R, 2, 2], U32)

        def const(name, rows_=R):
            a, b = CONST[name]
            return cst[0:rows_, a:b]

        def landed(b, par, dmas=1):
            return 8 * dmas * (b - par) + 16 * dmas

        def wait_count(eng, s, count):
            if not isinstance(count, int) or count > 0:
                eng.wait_ge(s, count)

        N_WTS = 10
        block = ctx.enter_context(nc.Block())

        def apart(eng):
            eng.wait_ge(sem["const_in"], 16)

        @block.sync
        def _(sp):
            sp.dma_start(cst[:, :], consts).then_inc(sem["const_in"], 16)
            sp.dma_start(tokw[:, :, :], tok_w).then_inc(sem["wts_in"], 16)

            def load_front(b, par):
                wait_count(sp, sem["emb_ps"], b - 1)
                sp.dma_start(xpat[:, par], patches[bass.ds(b, 1)].rearrange("o p k l -> (o p) k l")
                             ).then_inc(sem["patch_in"][par], 16)
                wait_count(sp, sem["h1"], b - 1)
                t = txt[bass.ds(b, 1)].rearrange("o t d -> (o t) d")
                sp.dma_start(h[IMG:R, par, 0, :], t[0:R - IMG]).then_inc(sem["text_in"][par], 16)
                sp.dma_start(h[0:N - R, par, 1, :], t[R - IMG:TXT]).then_inc(sem["text_in"][par], 16)

            def store_back(b, par):
                wait_count(sp, sem["h1"], b + 1)
                o = out[bass.ds(b, 1)].rearrange("o t d -> (o t) d")
                sp.dma_start(o[0:R], rows[0:R, par, 0, 0:D]).then_inc(sem["h1_stored"][par], 16)
                sp.dma_start(o[R:N], rows[0:N - R, par, 1, 0:D]).then_inc(sem["h1_stored"][par], 16)
                if not isinstance(b, int) or b > 0:
                    sp.wait_ge(sem["h1_stored"][1 - par], landed(b - 1, 1 - par, 2))
                    sp.sem_inc(sem["rows_stored"], 1)

            sp.wait_ge(sem["zero_set"], 1)
            load_front(0, 0)
            sp.dma_start(bias[:, :], tok_b.partition_broadcast(IMG)).then_inc(sem["bias_in"], 16)
            for dst, src in ((wfg[:, :, :], wfg1), (wqs[:, :, :], wq), (wks[:, :, :], wk), (wf2s[:, :], wf2),
                             (wvs[:, :, :], wv), (wg2s[DK:2 * DK, :], wg2), (wos[:, :, :], wo), (nw[:, :], norm_w),
                             (wrs[:, :, :], wr)):
                sp.dma_start(dst, src).then_inc(sem["wts_in"], 16)
            load_front(1, 1)
            for c in range(ZC):
                sp.dma_start(table.rearrange("(c r a) d -> c r (a d)", c=ZC, r=R)[c], zero[:, :]
                             ).then_inc(sem["table_clear"], 16)
            for e in range(2):
                sp.dma_start(w1s[:, e], w1[e]).then_inc(sem["w1_in"][e], 16)
                sp.dma_start(w2s[:, e], w2[e]).then_inc(sem["w2_in"][e], 16)
            sp.sem_inc(sem["rows_stored"], 1)
            store_back(0, 0)
            with sp.Fori(1, B // 2) as pair:
                i = 2 * pair
                load_front(i, 0)
                store_back(i - 1, 1)
                load_front(i + 1, 1)
                store_back(i, 0)
            store_back(B - 1, 1)

            def load_rows(e, par):
                wait_count(sp, sem["yout"], e - 1)
                t = table.rearrange("(e t r) d -> e r t d", e=E, t=2)[bass.ds(e, 1)]
                sp.dma_start(er[:, par], t.rearrange("o r t d -> (o r) t d")).then_inc(sem["rows_in"][par], 16)

            def load_weights(e, par):
                wait_count(sp, sem["hid_ps"], 4 * (e - 1))
                sp.dma_start(w1s[:, par], w1[bass.ds(e, 1)].rearrange("o p k f -> (o p) k f")
                             ).then_inc(sem["w1_in"][par], 16)
                wait_count(sp, sem["ye_ps"], e - 1)
                sp.dma_start(w2s[:, par], w2[bass.ds(e, 1)].rearrange("o p k f -> (o p) k f")
                             ).then_inc(sem["w2_in"][par], 16)

            for par in range(2):
                sp.wait_ge(sem["table_io"][par], 16 * B)
            load_rows(0, 0)
            load_rows(1, 1)
            with sp.Fori(1, E // 2) as pair:
                e = 2 * pair
                load_weights(e, 0)
                load_rows(e, 0)
                load_weights(e + 1, 1)
                load_rows(e + 1, 1)
            for par in range(2):
                sp.wait_ge(sem["out_rows"][par], 16 * E)
                sp.wait_ge(sem["h1_stored"][par], 16 * B)

        @block.tensor
        def _(pe):
            ident = const("ident", P)

            def mm(o, lhsT, rhs, start=True, stop=True):
                return nc.tensor.matmul(o, lhsT, rhs, start=start, stop=stop)

            def embed(b, par):
                pe.wait_ge(sem["patch_in"][par], landed(b, par))
                wait_count(pe, sem["ST"], b)
                for k in range(KP):
                    x = mm(psF[0:IMG, 0, 0:D], xpat[:, par, k, :], tokw[:, k, :], k == 0, k == KP - 1)
                x.then_inc(sem["emb_ps"], 1)

            def turn_xn(b):
                pe.wait_ge(sem["xn"], b + 1)
                for t in range(2):
                    for k in range(KD):
                        x = nc.tensor.transpose(psF[:, 1, k * 2 * R + t * R:k * 2 * R + (t + 1) * R],
                                                xn[:, t, k * P:(k + 1) * P], const("ident")[:, 0:R])
                x.then_inc(sem["xnT_ps"], 1)

            def project_fg_qk(b):
                pe.wait_ge(sem["xnT"], b + 1)
                pe.wait_ge(sem["h_img"], b + 1)
                for k in range(KD):
                    x = mm(psF[0:2 * DK, 0, 0:2 * R], wfg[:, k, :], xnT[:, k, :], k == 0, k == KD - 1)
                x.then_inc(sem["fg_ps"], 1)
                for w, bank in ((wqs, 2), (wks, 3)):
                    for c in range(KD):
                        for k in range(KD):
                            x = mm(psF[:, bank, c * 2 * R:(c + 1) * 2 * R], w[:, k, c * P:(c + 1) * P],
                                   xnT[:, k, :], k == 0, k == KD - 1)
                x.then_inc(sem["qk_ps"], 1)

            def forget_gates(b):
                pe.wait_ge(sem["fgT"], b + 1)
                for t in range(2):
                    x = mm(psF[0:R, t, :], fgT[0:DK, t * R:(t + 1) * R], wf2s[:, :])
                x.then_inc(sem["f_ps"], 1)

            def values_gate(b):
                pe.wait_ge(sem["qkT"], b + 1)
                for t in range(2):
                    for k in range(KD):
                        x = mm(psF[0:R, 2, t * D:(t + 1) * D], xnT[:, k, t * R:(t + 1) * R], wvs[:, k, :],
                               k == 0, k == KD - 1)
                x.then_inc(sem["v_ps"], 1)
                for t in range(2):
                    x = mm(psF[0:R, 3, t * D:(t + 1) * D], fgT[DK:2 * DK, t * R:(t + 1) * R],
                           wg2s[DK:2 * DK, :])
                x.then_inc(sem["g_ps"], 1)

            def decays(b):
                pe.wait_ge(sem["logf"], b + 1)
                for t in range(2):
                    x = mm(psF[0:R, t, :], const("centre"), logf[:, t, :])
                x.then_inc(sem["d_ps"], 1)
                pe.wait_ge(sem["v"], b + 1)
                mm(psF[0:R, 2, :], const("cross0"), logf[:, 0, :], True, False)
                mm(psF[0:R, 2, :], const("cross1"), logf[:, 1, :], False, True).then_inc(sem["e_ps"], 1)

            def turn_slots(b, par):
                pe.wait_ge(sem["S_rows"], b + 1)
                pe.wait_ge(sem["eD"], b + 1)
                pe.wait_ge(sem["g_lsg"], b + 1)
                for hp in range(4):
                    for a in range(3):
                        x = nc.tensor.transpose(psF[:, hp, a * R:(a + 1) * R], S[:, par, a, hp * P:(hp + 1) * P],
                                                const("ident")[:, 0:R])
                x.then_inc(sem["ST_ps"], 1)

            def qk_products(b, par, half, done):
                for r in range(4):
                    q = qkT[r * DK:(r + 1) * DK, par, 0, half, :]
                    kk = qkT[r * DK:(r + 1) * DK, par, 1, half, :]
                    mm(psB[0:R, r, 0:2 * R], kk[:, 0:R], q)
                    x = mm(psB[0:R, r, 2 * R:3 * R], kk[:, R:2 * R], q[:, R:2 * R])
                x.then_inc(done, 1)

            def slot_scores(b, par):
                pe.wait_ge(sem["pb"], b + 1)
                for hh in range(H):
                    m = slice(hh * M, (hh + 1) * M)
                    mm(psB[0:R, 0, m], PT[:, hh, 0:R], S[:, par, 0, m])
                    mm(psB[0:R, 1, m], PT[:, hh, R:2 * R], S[:, par, 1, m], True, False)
                    x = mm(psB[0:R, 1, m], PT[:, hh, 2 * R:3 * R], S[:, par, 2, m], False, True)
                x.then_inc(sem["o_ps"], 1)

            def turn_QE(b):
                pe.wait_ge(sem["QE"], b + 1)
                for hp in range(4):
                    for t in range(2):
                        at = (hp % 2) * 2 * R + t * R
                        x = nc.tensor.transpose(psB[:, 2 + hp // 2, at:at + R], QE[:, t, hp * P:(hp + 1) * P],
                                                const("ident")[:, 0:R])
                x.then_inc(sem["QET_ps"], 1)

            def slot_weights(b, par, half, done):
                for r in range(4):
                    hh = 4 * half + r
                    ps = slice((hh % 2) * M, (hh % 2 + 1) * M)
                    qe, st = QET[ps, hh // 2, :], ST[ps, par, hh // 2, :]
                    mm(psB[0:R, r, R:2 * R], st[:, R:2 * R], qe[:, R:2 * R])
                    for k0, q0 in ((0, 0), (2 * R, R)):
                        mm(psB[0:CUT, r, k0:k0 + CUT], st[:, k0:k0 + CUT], qe[:, q0:q0 + CUT])
                        x = mm(psB[0:R, r, k0 + CUT:k0 + R], st[:, k0:k0 + R], qe[:, q0 + CUT:q0 + R])
                x.then_inc(done, 1)

            def mix_values(b, par):
                pe.wait_ge(sem["ab"], b + 1)
                for hh in range(H):
                    c = slice(hh * DK, (hh + 1) * DK)
                    mm(psB[0:R, 0, c], AT[:, hh, 0:R], v[:, par, 0, c])
                    o1 = psB[0:R, 0, D + hh * DK:D + (hh + 1) * DK]
                    mm(o1, AT[:, hh, R:2 * R], v[:, par, 0, c], True, False)
                    x = mm(o1, AT[:, hh, 2 * R:3 * R], v[:, par, 1, c], False, True)
                x.then_inc(sem["ov_ps"], 1)

            def turn(src, bank, ready, done, b, ps):
                pe.wait_ge(ready, b + 1)
                for t in range(2):
                    for k in range(KD):
                        x = nc.tensor.transpose(ps[:, bank, k * 2 * R + t * R:k * 2 * R + (t + 1) * R],
                                                src[:, t, k * P:(k + 1) * P], const("ident")[:, 0:R])
                x.then_inc(done, 1)

            def output_projection(b):
                pe.wait_ge(sem["ogT"], b + 1)
                for t in range(2):
                    for k in range(KD):
                        x = mm(psB[0:R, 2, t * D:(t + 1) * D], ogT[:, k, t * R:(t + 1) * R], won[:, k, :],
                               k == 0, k == KD - 1)
                x.then_inc(sem["wo_ps"], 1)

            def logits(b):
                pe.wait_ge(sem["xfT"], b + 1)
                for t in range(2):
                    for k in range(KD):
                        x = mm(psB[0:R, 0, t * E:(t + 1) * E], xfT[:, k, t * R:(t + 1) * R], wrs[:, k, :],
                               k == 0, k == KD - 1)
                x.then_inc(sem["lg_ps"], 1)

            def ranks(b):
                pe.wait_ge(sem["ohv"], b + 1)
                wait_count(pe, sem["acc2"], b)
                before, ones = const("before"), const("ones")
                mm(psB[0:R, 1, 0:E], before, oh[:, 0, :], True, False)
                mm(psB[0:R, 1, 0:E], ones, acc[:, :], False, True)
                mm(psB[0:R, 1, E:2 * E], before, oh[:, 1, :], True, False)
                mm(psB[0:R, 1, E:2 * E], ones, oh[:, 0, :], False, False)
                mm(psB[0:R, 1, E:2 * E], ones, acc[:, :], False, True).then_inc(sem["rank_ps"], 1)

            def step(i, par, front=True, back=True):
                b, bp = i - 1, 1 - par
                if front:
                    embed(i, par)
                if back:
                    wait_count(pe, sem["slot"], b)
                    wait_count(pe, sem["xfT"], b)
                    wait_count(pe, sem["h1"], b)
                    qk_products(b, bp, 0, sem["pa_ps"])
                if front:
                    turn_xn(i)
                if back:
                    pe.wait_ge(sem["pa"], b + 1)
                    qk_products(b, bp, 1, sem["pb_ps"])
                if front:
                    project_fg_qk(i)
                if back:
                    slot_scores(b, bp)
                if front:
                    forget_gates(i)
                    values_gate(i)
                if back:
                    turn_QE(b)
                if front:
                    decays(i)
                if back:
                    pe.wait_ge(sem["QET"], b + 1)
                    slot_weights(b, bp, 0, sem["aa_ps"])
                    pe.wait_ge(sem["aa"], b + 1)
                    slot_weights(b, bp, 1, sem["ab_ps"])
                if front:
                    turn_slots(i, par)
                if back:
                    mix_values(b, bp)
                    turn(og, 1, sem["og"], sem["ogT_ps"], b, psB)
                    output_projection(b)
                    turn(xf, 3, sem["xf"], sem["xfT_ps"], b, psB)
                    logits(b)
                    ranks(b)

            pe.wait_ge(sem["const_in"], 16)
            pe.wait_ge(sem["wts_in"], 16 * N_WTS)
            step(0, 0, back=False)
            pe.wait_ge(sem["wo_scaled"], 1)
            step(1, 1)
            with pe.Fori(1, B // 2) as pair:
                i = 2 * pair
                step(i, 0)
                step(i + 1, 1)
            step(B, 0, front=False)

            def expert(e, par):
                turn(xe, 0, sem["xe_rows"], sem["xeT_ps"], e, psB)
                pe.wait_ge(sem["w1_in"][par], landed(e, par))
                pe.wait_ge(sem["xeT"], e + 1)
                for g in range(4):
                    wait_count(pe, sem["hid"], 4 * e + g)
                    for f in range(2):
                        for k in range(KD):
                            c = (2 * g + f) * P
                            x = mm(psF[:, g % 2, f * SLOTS:(f + 1) * SLOTS], w1s[:, par, k, c:c + P], xeT[:, k, :],
                                   k == 0, k == KD - 1)
                    x.then_inc(sem["hid_ps"], 1)
                pe.wait_ge(sem["w2_in"][par], landed(e, par))
                pe.wait_ge(sem["hid"], 4 * (e + 1))
                for c in range(KD):
                    for k in range(KF):
                        x = mm(psB[:, 1, c * SLOTS:(c + 1) * SLOTS], w2s[:, par, k, c * P:(c + 1) * P], hid[:, k, :],
                               k == 0, k == KF - 1)
                x.then_inc(sem["ye_ps"], 1)
                pe.wait_ge(sem["yeT"], e + 1)
                wait_count(pe, sem["yout"], e)
                for t in range(2):
                    for c in range(KD):
                        x = nc.tensor.transpose(psB[0:R, 2, t * D + c * P:t * D + (c + 1) * P],
                                                yeT[:, c, t * R:(t + 1) * R], ident)
                x.then_inc(sem["yb_ps"], 1)

            pe.wait_ge(sem["ST"], B)
            expert(0, 0)
            expert(1, 1)
            with pe.Fori(1, E // 2) as pair:
                e = 2 * pair
                expert(e, 0)
                expert(e + 1, 1)

        @block.scalar
        def _(act):
            nc.scalar.preload_act_table_set("natural_log_exp_and_others")

            def fn(o, i, f, done, **kw):
                return nc.scalar.activation(o, i, f, **kw).then_inc(done, 1)

            def front1(b):
                act.wait_ge(sem["xnT_ps"], b + 1)
                fn(xnT[:, :, :].rearrange("p k t -> p (k t)"), psF[:, 1, 0:4 * R], ACT.Copy, sem["xnT"])

            def front2(b):
                act.wait_ge(sem["qk_ps"], b + 1)
                wait_count(act, sem["q_sig"], b)
                fn(qab[:, :, :], psF[:, 2:4, 0:4 * R], ACT.Abs, sem["q_abs"])
                act.wait_ge(sem["q_abs"], b + 1)
                fn(qab[:, :, :], qab[:, :, :], ACT.Exp, sem["q_exp"], scale=-1.0)
                act.wait_ge(sem["q_exp"], b + 1)
                fn(qln[:, :, :], qab[:, :, :], ACT.Ln, sem["q_ln"], bias=1.0)

            def front3(b):
                act.wait_ge(sem["f_ps"], b + 1)
                fn(fab[:, :, :], psF[0:R, 0:2, :], ACT.Abs, sem["f_abs"])
                act.wait_ge(sem["f_abs"], b + 1)
                fn(fab[:, :, :], fab[:, :, :], ACT.Exp, sem["f_exp"], scale=-1.0)
                act.wait_ge(sem["f_exp"], b + 1)
                fn(fab[:, :, :], fab[:, :, :], ACT.Ln, sem["f_ln"], bias=1.0)
                act.wait_ge(sem["q_lsg"], b + 1)
                fn(qab[:, :, :], qln[:, :, :], ACT.Exp, sem["q_sig"])

            def front4(b, par):
                act.wait_ge(sem["logf"], b + 1)
                wait_count(act, sem["s"], b)
                fn(sig[:, :, :], logf[:, :, :], ACT.Exp, sem["f_sig"])
                act.wait_ge(sem["g_ps"], b + 1)
                fn(gab[:, :], psF[0:R, 3, :], ACT.Abs, sem["g_abs"])
                act.wait_ge(sem["g_abs"], b + 1)
                fn(gab[:, :], gab[:, :], ACT.Exp, sem["g_exp"], scale=-1.0)
                act.wait_ge(sem["g_exp"], b + 1)
                fn(gab[:, :], gab[:, :], ACT.Ln, sem["g_ln"], bias=1.0)

            def front5(b, par):
                act.wait_ge(sem["d_ps"], b + 1)
                wait_count(act, sem["S_rows"], b)
                fn(ek[:, 0::2, :], psF[0:R, 0:2, :], ACT.Exp, sem["ekD"], scale=-1.0)
                act.wait_ge(sem["e_ps"], b + 1)
                fn(ek[:, 1, :], psF[0:R, 2, :], ACT.Exp, sem["ecD"])
                wait_count(act, sem["QE"], b - 1)
                fn(eD[:, par], psF[0:R, 0:2, :], ACT.Exp, sem["eD"])
                act.wait_ge(sem["g_lsg"], b + 1)
                wait_count(act, sem["ogn"], b - 1)
                fn(sg[:, par], gab[:, :], ACT.Exp, sem["g_sig"])

            def back1(b):
                act.wait_ge(sem["umx"], b + 1)
                fn(pexp[:, :, :], um[:, :, :], ACT.Exp, sem["pexp"])

            def back2(b):
                act.wait_ge(sem["QET_ps"], b + 1)
                fn(QET[:, 0:4, :].rearrange("p (a c) t -> p a (c t)", a=2), psB[:, 2:4, 0:4 * R], ACT.Copy, sem["QET"])

            def back3(b):
                act.wait_ge(sem["ogn"], b + 1)
                fn(sq[:, :, :], ogn[:, :, :], ACT.Square, sem["sq"])

            def copy_T(b, dst, bank, ready, done, ps=psB):
                act.wait_ge(ready, b + 1)
                fn(dst[:, :, :].rearrange("p k t -> p (k t)"), ps[:, bank, 0:4 * R], ACT.Copy, done)

            def back6(b):
                act.wait_ge(sem["ldm"], b + 1)
                fn(rt[:, 1, :], rt[:, 0, :], ACT.Exp, sem["lexp"])

            def step(i, par, front=True, back=True):
                b = i - 1
                if front:
                    front1(i)
                    front2(i)
                if front:
                    front3(i)
                if back:
                    back1(b)
                if front:
                    front4(i, par)
                if back:
                    back2(b)
                if front:
                    front5(i, par)
                if back:
                    back3(b)
                    copy_T(b, ogT, 1, sem["ogT_ps"], sem["ogT"])
                    copy_T(b, xfT, 3, sem["xfT_ps"], sem["xfT"])
                    back6(b)

            step(0, 0, back=False)
            step(1, 1)
            with act.Fori(1, B // 2) as pair:
                i = 2 * pair
                step(i, 0)
                step(i + 1, 1)
            step(B, 0, front=False)

            def expert(e, par):
                copy_T(e, xeT, 0, sem["xeT_ps"], sem["xeT"])
                for g in range(4):
                    act.wait_ge(sem["hid_ps"], 4 * e + g + 1)
                    if g == 0:
                        wait_count(act, sem["ye_ps"], e)
                    fn(hid[:, 2 * g:2 * g + 2, :].rearrange("p f t -> p (f t)"), psF[:, g % 2, 0:4 * R],
                       ACT.Relu, sem["hid"])
                act.wait_ge(sem["ye_ps"], e + 1)
                fn(yeT[:, :, :].rearrange("p k t -> p (k t)"), psB[:, 1, 0:4 * R], ACT.Copy, sem["yeT"])

            expert(0, 0)
            expert(1, 1)
            with act.Fori(1, E // 2) as pair:
                e = 2 * pair
                expert(e, 0)
                expert(e + 1, 1)

        @block.vector
        def _(dve):
            v3 = "r t (h m) -> r (t h) m"

            def tt(o, a, b_, op, done):
                return nc.vector.tensor_tensor(o, a, b_, op).then_inc(done, 1)

            def front1(b, par):
                dve.wait_ge(sem["emb_ps"], b + 1)
                dve.wait_ge(sem["text_in"][par], landed(b, par, 2))
                wait_count(dve, sem["h1"], b - 1)
                tt(h[0:IMG, par, 0, :], psF[0:IMG, 0, 0:D], bias[:, :], ALU.add, sem["h_img"])
                dve.wait_ge(sem["h_img"], b + 1)
                for t in range(2):
                    x = nc.vector.bn_stats(st1[:, t, :], h[:, par, t, :])
                x.then_inc(sem["stats1"], 1)
                apart(dve)
                dve.wait_ge(sem["stats1"], b + 1)
                for t in range(2):
                    x = nc.vector.bn_aggr(mv1[:, t, :], st1[:, t, :])
                x.then_inc(sem["mv1"], 1)
                dve.wait_ge(sem["rstd1"], b + 1)
                wait_count(dve, sem["xnT_ps"], b)
                for t in range(2):
                    x = nc.vector.tensor_scalar(xn[:, t, :], h[:, par, t, :], mv1[:, t, 0:1], rs1[:, t:t + 1],
                                                ALU.subtract, ALU.mult)
                x.then_inc(sem["xn"], 1)

            def front2(b, par):
                dve.wait_ge(sem["fg_ps"], b + 1)
                nc.vector.tensor_copy(fgT[:, :], psF[0:2 * DK, 0, 0:2 * R]).then_inc(sem["fgT"], 1)
                dve.wait_ge(sem["q_ln"], b + 1)
                nc.vector.scalar_tensor_tensor(out=qln[:, :, :], in0=psF[:, 2:4, 0:4 * R], scalar=0.0,
                                               in1=qln[:, :, :], op0=ALU.min, op1=ALU.subtract
                                               ).then_inc(sem["q_lsg"], 1)

            def front3(b, par):
                dve.wait_ge(sem["f_ln"], b + 1)
                wait_count(dve, sem["e_ps"], b)
                nc.vector.scalar_tensor_tensor(out=logf[:, :, :], in0=psF[0:R, 0:2, :], scalar=0.0,
                                               in1=fab[:, :, :], op0=ALU.min, op1=ALU.subtract
                                               ).then_inc(sem["logf"], 1)
                dve.wait_ge(sem["q_sig"], b + 1)
                wait_count(dve, sem["pb_ps"], b - 1)
                tt(qkT[:, par].rearrange("p a k t -> p a (k t)"), psF[:, 2:4, 0:4 * R], qab[:, :, :],
                   ALU.mult, sem["qkT"])

            def front4(b, par):
                dve.wait_ge(sem["v_ps"], b + 1)
                wait_count(dve, sem["ov_ps"], b - 1)
                nc.vector.tensor_copy(v[:, par].rearrange("r t d -> r (t d)"), psF[0:R, 2, :]).then_inc(sem["v"], 1)
                dve.wait_ge(sem["g_ln"], b + 1)
                wait_count(dve, sem["g_sig"], b)
                nc.vector.scalar_tensor_tensor(out=gab[:, :], in0=psF[0:R, 3, :], scalar=0.0, in1=gab[:, :],
                                               op0=ALU.min, op1=ALU.subtract).then_inc(sem["g_lsg"], 1)

            def front5(b, par):
                dve.wait_ge(sem["ST_ps"], b + 1)
                wait_count(dve, sem["ab_ps"], b - 1)
                nc.vector.tensor_copy(ST[:, par], psF[:, 0:4, 0:3 * R]).then_inc(sem["ST"], 1)

            def mask_P(b, half, ready, done):
                dve.wait_ge(ready, b + 1)
                tt(PT[:, 4 * half:4 * half + 4, :], psB[0:R, 0:4, 0:3 * R],
                   const("mask").unsqueeze(1).to_broadcast([R, 4, 3 * R]), ALU.mult, done)

            def mask_A(b, half, ready, done):
                dve.wait_ge(ready, b + 1)
                nc.vector.scalar_tensor_tensor(
                    out=AT[:, 4 * half:4 * half + 4, :], in0=psB[0:R, 0:4, 0:3 * R], scalar=ABIG,
                    in1=const("mask").unsqueeze(1).to_broadcast([R, 4, 3 * R]), op0=ALU.min, op1=ALU.mult
                    ).then_inc(done, 1)

            def softmax1(b, par):
                dve.wait_ge(sem["o_ps"], b + 1)
                wait_count(dve, sem["QE"], b)
                tt(u[:, :, :], psB[0:R, 0:2, :], eD[:, par], ALU.mult, sem["u"])
                dve.wait_ge(sem["u"], b + 1)
                nc.vector.tensor_reduce(mx[:, :], u[:, :, :].rearrange("r t (h m) -> r (t h) m", m=M), AX_X,
                                        ALU.max).then_inc(sem["umax"], 1)
                dve.wait_ge(sem["umax"], b + 1)
                tt(um[:, :, :].rearrange("r t (h m) -> r (t h) m", m=M),
                   u[:, :, :].rearrange("r t (h m) -> r (t h) m", m=M),
                   mx[:, :].unsqueeze(2).to_broadcast([R, 2 * H, M]), ALU.subtract, sem["umx"])

            def softmax2(b):
                dve.wait_ge(sem["pexp"], b + 1)
                nc.vector.tensor_reduce(Z[:, :], pexp[:, :, :].rearrange("r t (h m) -> r (t h) m", m=M), AX_X,
                                        ALU.add).then_inc(sem["Z"], 1)
                dve.wait_ge(sem["Z"], b + 1)
                nc.vector.reciprocal(rZ[:, :], Z[:, :]).then_inc(sem["rZ"], 1)
                dve.wait_ge(sem["rZ"], b + 1)
                tt(rz2[:, :], rZ[:, :], rZ[:, :], ALU.mult, sem["rz2"])

            def heads(x):
                return x.rearrange("r t (h c) -> r (t h) c", c=DK)

            def attention_out(b, par):
                dve.wait_ge(sem["ov_ps"], b + 1)
                dve.wait_ge(sem["g_sig"], b + 1)
                wait_count(dve, sem["og"], b)
                tt(ogn[:, :, :].rearrange("r t d -> r (t d)"), psB[0:R, 0, :], sg[:, par], ALU.mult, sem["ogn"])
                dve.wait_ge(sem["sq"], b + 1)
                nc.vector.tensor_reduce(ss[:, 0, :], heads(sq[:, :, :]), AX_X, ALU.add).then_inc(sem["ss"], 1)
                dve.wait_ge(sem["ss"], b + 1)
                dve.wait_ge(sem["rz2"], b + 1)
                tt(ss[:, 1, :], ss[:, 0, :], rz2[:, :], ALU.mult, sem["ss2"])
                dve.wait_ge(sem["ss2"], b + 1)
                nc.vector.tensor_scalar(ss[:, 2, :], ss[:, 1, :], 1.0 / DK, RMS_EPS, ALU.mult, ALU.add
                                        ).then_inc(sem["ss3"], 1)

            def residual(b, par):
                dve.wait_ge(sem["wo_ps"], b + 1)
                wait_count(dve, sem["rows_stored"], b)
                wait_count(dve, sem["rows_dispatched"], b)
                tt(rows[:, par, :, 0:D], psB[0:R, 2, :].rearrange("r (t d) -> r t d", t=2), h[:, par], ALU.add,
                   sem["h1"])
                dve.wait_ge(sem["h1"], b + 1)
                for t in range(2):
                    x = nc.vector.bn_stats(st2[:, t, :], rows[:, par, t, 0:D])
                x.then_inc(sem["stats2"], 1)
                apart(dve)
                dve.wait_ge(sem["stats2"], b + 1)
                for t in range(2):
                    x = nc.vector.bn_aggr(mv2[:, t, :], st2[:, t, :])
                x.then_inc(sem["mv2"], 1)
                dve.wait_ge(sem["rstd2"], b + 1)
                nc.vector.scalar_tensor_tensor(out=rows[:, par, :, C_NMR], in0=mv2[:, :, 0], scalar=-1.0,
                                               in1=rows[:, par, :, C_RSTD], op0=ALU.mult, op1=ALU.mult
                                               ).then_inc(sem["nmr"], 1)
                dve.wait_ge(sem["nmr"], b + 1)
                for t in range(2):
                    x = nc.vector.tensor_scalar(xf[:, t, :], rows[:, par, t, 0:D], rows[:, par, t, C_RSTD:C_RSTD + 1],
                                                rows[:, par, t, C_NMR:C_NMR + 1], ALU.mult, ALU.add)
                x.then_inc(sem["xf"], 1)
                nc.vector.tensor_copy(rows[:, par, :, C_TOK], tokc[:, :]).then_inc(sem["tokset"], 1)
                dve.wait_ge(sem["tokset"], b + 1)
                nc.vector.tensor_scalar(tokc[:, :], tokc[:, :], float(N), None, ALU.add).then_inc(sem["toknext"], 1)

            def e3(x):
                return x.rearrange("r (t e) -> r t e", e=E)

            def route(b, par):
                def bc(x):
                    return x.unsqueeze(2).to_broadcast([R, 2, E])
                dve.wait_ge(sem["lg_ps"], b + 1)
                nc.vector.tensor_reduce(rsm[:, 0, :], e3(psB[0:R, 0, 0:2 * E]), AX_X, ALU.max
                                        ).then_inc(sem["lmax"], 1)
                dve.wait_ge(sem["lmax"], b + 1)
                tt(e3(rt[:, 0, :]), e3(psB[0:R, 0, 0:2 * E]), bc(rsm[:, 0, :]), ALU.subtract, sem["ldm"])
                dve.wait_ge(sem["ldm"], b + 1)
                nc.vector.scalar_tensor_tensor(out=rt[:, 2, :], in0=rt[:, 0, :], scalar=0.0, in1=const("rev"),
                                               op0=ALU.is_ge, op1=ALU.mult).then_inc(sem["pick"], 1)
                dve.wait_ge(sem["pick"], b + 1)
                nc.vector.tensor_reduce(rsm[:, 1, :], e3(rt[:, 2, :]), AX_X, ALU.max).then_inc(sem["pickmax"], 1)
                dve.wait_ge(sem["pickmax"], b + 1)
                tt(e3(rt[:, 3, :]), e3(const("rev")), bc(rsm[:, 1, :]), ALU.is_equal, sem["oh"])
                dve.wait_ge(sem["oh"], b + 1)
                wait_count(dve, sem["acc2"], b)
                tt(oh[:, :, :], e3(rt[:, 3, :]), e3(const("validE")), ALU.mult, sem["ohv"])
                dve.wait_ge(sem["lexp"], b + 1)
                nc.vector.tensor_reduce(rsm[:, 2, :], e3(rt[:, 1, :]), AX_X, ALU.add).then_inc(sem["lsum"], 1)
                dve.wait_ge(sem["lsum"], b + 1)
                nc.vector.reciprocal(rows[:, par, :, C_PROB], rsm[:, 2, :]).then_inc(sem["prob"], 1)
                dve.wait_ge(sem["rank_ps"], b + 1)
                nc.vector.tensor_scalar(rt[:, 4, :], psB[0:R, 1, 0:2 * E], float(CAP), FAR, ALU.is_ge, ALU.mult
                                        ).then_inc(sem["over"], 1)
                tt(rt[:, 5, :], psB[0:R, 1, 0:2 * E], const("ebase"), ALU.add, sem["eslot"])
                dve.wait_ge(sem["over"], b + 1)
                dve.wait_ge(sem["eslot"], b + 1)
                tt(rt[:, 6, :], rt[:, 4, :], rt[:, 5, :], ALU.add, sem["slotx"])
                dve.wait_ge(sem["slotx"], b + 1)
                dve.wait_ge(sem["ohv"], b + 1)
                tt(rt[:, 7, :], rt[:, 6, :], oh[:, :, :].rearrange("r t e -> r (t e)"), ALU.mult, sem["slotoh"])
                dve.wait_ge(sem["slotoh"], b + 1)
                nc.vector.tensor_reduce(rsm[:, 3, :], e3(rt[:, 7, :]), AX_X, ALU.add).then_inc(sem["slotsum"], 1)
                dve.wait_ge(sem["slotsum"], b + 1)
                tt(slot[:, par, :], rsm[:, 3, :], const("far"), ALU.add, sem["slot"])
                tt(acct[:, :], oh[:, 0, :], oh[:, 1, :], ALU.add, sem["acc1"])
                dve.wait_ge(sem["acc1"], b + 1)
                tt(acc[:, :], acc[:, :], acct[:, :], ALU.add, sem["acc2"])

            def step(i, par, front=True, back=True):
                b, bp = i - 1, 1 - par
                if front:
                    front1(i, par)
                if back:
                    mask_P(b, 0, sem["pa_ps"], sem["pa"])
                if back:
                    mask_P(b, 1, sem["pb_ps"], sem["pb"])
                if front:
                    front2(i, par)
                    front3(i, par)
                if back:
                    softmax1(b, bp)
                if front:
                    front4(i, par)
                if back:
                    softmax2(b)
                    mask_A(b, 0, sem["aa_ps"], sem["aa"])
                    mask_A(b, 1, sem["ab_ps"], sem["ab"])
                if front:
                    front5(i, par)
                if back:
                    attention_out(b, bp)
                    residual(b, bp)
                    route(b, bp)

            nc.vector.memset(h[64:R, :, 1, :], 0.0)
            nc.vector.memset(acc[:, :], 0.0)
            nc.vector.memset(halfH[:, :], -0.5)
            nc.vector.memset(zero[:, :], 0.0).then_inc(sem["zero_set"], 1)
            dve.wait_ge(sem["const_in"], 16)
            nc.vector.tensor_copy(tokc[:, :], const("tok")).then_inc(sem["zero_set"], 1)
            dve.wait_ge(sem["bias_in"], 16)
            dve.wait_ge(sem["zero_set"], 2)
            step(0, 0, back=False)
            dve.wait_ge(sem["wts_in"], 16 * N_WTS)
            for k in range(KD):
                x = nc.vector.tensor_scalar(won[:, k, :], wos[:, k, :], nw[:, k:k + 1], None, ALU.mult)
            x.then_inc(sem["wo_scaled"], 1)
            step(1, 1)
            with dve.Fori(1, B // 2) as pair:
                i = 2 * pair
                step(i, 0)
                step(i + 1, 1)
            step(B, 0, front=False)

            def expert(e, par):
                dve.wait_ge(sem["rows_in"][par], landed(e, par))
                wait_count(dve, sem["xeT_ps"], e)
                for t in range(2):
                    x = nc.vector.tensor_scalar(xe[:, t, :], er[:, par, t, 0:D], er[:, par, t, C_RSTD:C_RSTD + 1],
                                                er[:, par, t, C_NMR:C_NMR + 1], ALU.mult, ALU.add)
                x.then_inc(sem["xe_rows"], 1)
                wait_count(dve, sem["idx"], e)
                nc.vector.tensor_scalar(ix0[:, :], er[:, par, :, C_TOK], 0.0, FAR + 1.0, ALU.is_equal, ALU.mult
                                        ).then_inc(sem["idx0"], 1)
                dve.wait_ge(sem["idx0"], e + 1)
                wait_count(dve, sem["out_rows"][par], landed(e - 2, par, 2))
                nc.vector.scalar_tensor_tensor(out=ix[:, par, :], in0=er[:, par, :, C_TOK], scalar=-1.0,
                                               in1=ix0[:, :], op0=ALU.add, op1=ALU.add).then_inc(sem["idx"], 1)

            def expert_out(e, par):
                dve.wait_ge(sem["yb_ps"], e + 1)
                for t in range(2):
                    x = nc.vector.scalar_tensor_tensor(out=yo[:, par, t, :], in0=psB[0:R, 2, t * D:(t + 1) * D],
                                                       scalar=er[:, par, t, C_PROB:C_PROB + 1],
                                                       in1=er[:, par, t, 0:D], op0=ALU.mult, op1=ALU.add)
                x.then_inc(sem["yout"], 1)

            expert(0, 0)
            expert_out(0, 0)
            expert(1, 1)
            expert_out(1, 1)
            with dve.Fori(1, E // 2) as pair:
                e = 2 * pair
                expert(e, 0)
                expert_out(e, 0)
                expert(e + 1, 1)
                expert_out(e + 1, 1)

        @block.gpsimd
        def _(pool):
            def rstd(b, mv, ve, o, ready, mid, done):
                pool.wait_ge(ready, b + 1)
                nc.gpsimd.tensor_tensor(ve[:, :], mv[:, :, 1], const("lneps"), ALU.add).then_inc(mid, 1)
                pool.wait_ge(mid, b + 1)
                nc.gpsimd.tensor_tensor(o, ve[:, :], const("neghalf"), ALU.pow).then_inc(done, 1)

            def s_rows(b):
                pool.wait_ge(sem["f_sig"], b + 1)
                nc.gpsimd.tensor_tensor(srow[:, :, :], const("ones")[:, 0:1].unsqueeze(1).to_broadcast([R, 2, HM]),
                                        sig[:, :, :], ALU.subtract).then_inc(sem["s"], 1)

            def scale_slots(b, par):
                pool.wait_ge(sem["ekD"], b + 1)
                pool.wait_ge(sem["ecD"], b + 1)
                pool.wait_ge(sem["s"], b + 1)
                wait_count(pool, sem["o_ps"], b - 1)
                wait_count(pool, sem["ST_ps"], b - 1)
                nc.gpsimd.tensor_tensor(S[:, par, 0::2, :], srow[:, :, :], ek[:, 0::2, :], ALU.mult)
                nc.gpsimd.tensor_tensor(S[:, par, 1, :], srow[:, 0, :], ek[:, 1, :], ALU.mult
                                        ).then_inc(sem["S_rows"], 1)

            def scale_queries(b, par):
                pool.wait_ge(sem["pexp"], b + 1)
                wait_count(pool, sem["QET_ps"], b)
                nc.gpsimd.tensor_tensor(QE[:, :, :], pexp[:, :, :], eD[:, par], ALU.mult).then_inc(sem["QE"], 1)

            def normalise(b):
                pool.wait_ge(sem["ss3"], b + 1)
                nc.gpsimd.tensor_tensor(ss[:, 3, :], ss[:, 2, :], halfH[:, :], ALU.pow).then_inc(sem["ss4"], 1)
                pool.wait_ge(sem["ss4"], b + 1)
                pool.wait_ge(sem["rZ"], b + 1)
                nc.gpsimd.tensor_tensor(ss[:, 4, :], ss[:, 3, :], rZ[:, :], ALU.mult).then_inc(sem["ss5"], 1)
                pool.wait_ge(sem["ss5"], b + 1)
                pool.wait_ge(sem["ogn"], b + 1)
                wait_count(pool, sem["ogT_ps"], b)
                nc.gpsimd.tensor_tensor(og[:, :, :].rearrange("r t (h c) -> r (t h) c", c=DK),
                                        ogn[:, :, :].rearrange("r t (h c) -> r (t h) c", c=DK),
                                        ss[:, 4, :].unsqueeze(2).to_broadcast([R, 2 * H, DK]), ALU.mult
                                        ).then_inc(sem["og"], 1)

            def dispatch(b, par):
                pool.wait_ge(sem["slot"], b + 1)
                pool.wait_ge(sem["prob"], b + 1)
                pool.wait_ge(sem["tokset"], b + 1)
                pool.sem_inc(sem["go_dispatch"], 1)
                for t in range(2):
                    nc.gpsimd.indirect_dma_start(
                        out=table, out_offset=bass.IndirectOffsetOnAxis(ap=slot[:, par, t:t + 1], axis=0),
                        in_=rows[:, par, t, :], in_offset=None, bounds_check=E * SLOTS - 1, oob_is_err=False
                        ).then_inc(sem["table_io"][par], 16)
                if not isinstance(b, int) or b > 0:
                    pool.wait_ge(sem["table_io"][1 - par], landed(b - 1, 1 - par, 2))
                    pool.sem_inc(sem["rows_dispatched"], 1)

            def step(i, par, front=True, back=True):
                b, bp = i - 1, 1 - par
                if front:
                    rstd(i, mv1, ve1, rs1[:, :], sem["mv1"], sem["ve1"], sem["rstd1"])
                if back:
                    scale_queries(b, bp)
                if front:
                    s_rows(i)
                    scale_slots(i, par)
                if back:
                    normalise(b)
                    rstd(b, mv2, ve2, rows[:, bp, :, C_RSTD], sem["mv2"], sem["ve2"], sem["rstd2"])
                    dispatch(b, bp)

            pool.wait_ge(sem["const_in"], 16)
            pool.wait_ge(sem["zero_set"], 1)
            pool.sem_inc(sem["rows_dispatched"], 1)
            step(0, 0, back=False)
            pool.wait_ge(sem["table_clear"], 16 * ZC)
            step(1, 1)
            with pool.Fori(1, B // 2) as pair:
                i = 2 * pair
                step(i, 0)
                step(i + 1, 1)
            step(B, 0, front=False)

            out_rows = out.rearrange("b n d -> (b n) d")
            def scatter(e, par):
                wait_count(pool, sem["yout"], e + 1)
                wait_count(pool, sem["idx"], e + 1)
                pool.sem_inc(sem["go_scatter"], 1)
                for t in range(2):
                    nc.gpsimd.indirect_dma_start(
                        out=out_rows, out_offset=bass.IndirectOffsetOnAxis(ap=ix[:, par, t:t + 1], axis=0),
                        in_=yo[:, par, t, :], in_offset=None, bounds_check=B * N - 1, oob_is_err=False
                        ).then_inc(sem["out_rows"][par], 16)

            for par in range(2):
                pool.wait_ge(sem["h1_stored"][par], 16 * B)
            scatter(0, 0)
            scatter(1, 1)
            with pool.Fori(1, E // 2) as pair:
                e = 2 * pair
                scatter(e, 0)
                scatter(e + 1, 1)


def shape_constants():
    c = np.zeros((P, CONST_COLS), np.float32)

    def put(name, a):
        lo, hi = CONST[name]
        c[:a.shape[0], lo:hi] = a

    i, t = np.arange(R)[:, None], np.arange(R)[None, :]
    tri = (i <= t)
    put("ident", np.eye(P))
    put("mask", np.concatenate([tri, np.ones((R, R)), tri], 1))
    put("centre", (i <= t).astype(np.float32) - (i <= MID))
    put("cross0", i > t)
    put("cross1", np.broadcast_to(i <= MID, (R, R)))
    put("before", i < t)
    put("ones", np.ones((R, R)))
    put("rev", np.tile(E - np.arange(E), (R, 2)))
    put("ebase", np.tile(SLOTS * np.arange(E), (R, 2)))
    real = np.ones((R, 2)); real[R - 1, 1] = 0
    put("valid", real)
    put("validE", np.repeat(real, E, axis=1))
    put("far", (1 - real) * FAR)
    put("tok", np.arange(R)[:, None] + np.array([[1, R + 1]]))
    put("neghalf", np.full((R, 2), -0.5))
    put("lneps", np.full((R, 2), LN_EPS))
    return c


def kernel(**inputs):
    import concourse.bacc as bacc
    from concourse.bass_utils import run_bass_kernel_spmd

    a = {k: np.asarray(x) for k, x in inputs.items()}

    def tiles(w):
        return w.reshape(-1, P, w.shape[-1]).transpose(1, 0, 2)

    patches = a["x"].reshape(B, 3, 7, PATCH, 7, PATCH).transpose(0, 2, 4, 1, 3, 5).reshape(B, IMG, KP, P)
    laid = {
        "patches": patches.transpose(0, 3, 2, 1),
        "txt": a["txt"],
        "tok_w": tiles(a["L0_tok_W"].T),
        "tok_b": a["L0_tok_b"],
        "wq": tiles(a["L0_attn_Wq"]), "wk": tiles(a["L0_attn_Wk"]), "wv": tiles(a["L0_attn_Wv"]),
        "wfg1": tiles(np.concatenate([a["L0_attn_Wf1"], a["L0_attn_Wg1"]], 1)),
        "wf2": a["L0_attn_Wf2"], "wg2": a["L0_attn_Wg2"], "wo": tiles(a["L0_attn_Wo"]),
        "norm_w": a["L0_attn_norm_w"].reshape(KD, P).T,
        "wr": tiles(a["L0_ffn_Wr"]),
        "w1": a["L0_ffn_W1"].reshape(E, KD, P, F).transpose(0, 2, 1, 3),
        "w2": a["L0_ffn_W2"].reshape(E, KF, P, D).transpose(0, 2, 1, 3),
        "consts": shape_constants(),
    }
    nc = bacc.Bacc("TRN2", target_bir_lowering=False, num_devices=1)
    arrays, args = {}, []
    for name, x in laid.items():
        x = np.ascontiguousarray(x)
        arrays["in_" + name] = x
        args.append(nc.dram_tensor("in_" + name, x.shape, mybir.dt.from_np(x.dtype), kind="ExternalInput").ap())
    args.append(nc.dram_tensor("out", (B, N, D), F32, kind="ExternalOutput").ap())
    program(nc, *args)
    r = run_bass_kernel_spmd(nc, [arrays], core_ids=[0])
    return r.results[0]["out"]
```

```python
from contextlib import ExitStack

import numpy as np
import concourse.bass as bass
from concourse import mybir

ALU = mybir.AluOpType
ACT = mybir.ActivationFunctionType
F32 = mybir.dt.float32
U32 = mybir.dt.uint32
AX_X = mybir.AxisListType.X

P = 128
B = 8
IMG = 49
TXT = 128
N = IMG + TXT
R = (N + 1) // 2
PATCH = 16
PD = 3 * PATCH * PATCH
KP = PD // P
D = 256
KD = D // P
H, M, DK = 8, 64, 32
HM = H * M
F = 1024
KF = F // P
E = 8
CAP = B * N // E
SLOTS = 2 * R
MID = R // 2
CUT = 64
LN_EPS = 1e-5
RMS_EPS = 1e-5
FAR = 8192.0
ZC = 8
COLS = D + 4
C_NMR, C_RSTD, C_TOK, C_PROB = D, D + 1, D + 2, D + 3
ABIG = 1e30

CONST = {}
_at = 0
for _name, _w in (("ident", P), ("mask", 2 * R), ("centre", R), ("cross0", R), ("cross1", R), ("before", R),
                  ("ones", R), ("rev", 2 * E), ("ebase", 2 * E), ("valid", 2), ("far", 2), ("tok", 2),
                  ("neghalf", 2), ("lneps", 2), ("zero", D), ("validE", 2 * E)):
    CONST[_name] = (_at, _at + _w)
    _at += _w
CONST_COLS = _at

PAIRED = "text_in table_io h1_stored out_rows w1_in w2_in rows_in res_in".split()
SEMS = """const_in emb_in wts_in table_clear zero_set rows_stored embT_ps embT img_kept
 emb_ps h_img stats1 mv1 ve1 rstd1 xn xnT_ps xnT fg_ps fgT qk_ps f_ps v_ps g_ps
 q_abs q_exp q_ln q_lsg q_sig qkT f_abs f_exp f_ln logf f_sig s g_abs g_exp g_ln g_lsg g_sig v
 d_ps e_ps eD ekD ecD S_rows ST_ps ST h_kept
 p_ps p_kept o_ps u umax umx pexp Z rZ rz2 QE QET_ps QETa QETb a_ps a_kept ov_ps ogn
 sq ss ss2 ss3 ss_ln rms scale og ogT_ps ogT wo_ps h1 stats2 mv2 ve2 rstd2 nmr xf xfT_ps xfT
 lg_ps lmax ldm lexp lsum prob pick pickmax oh ohv rank_ps over eslot slotx slotoh slotsum slot acc1 acc2
 tokset toknext wo_scaled go_dispatch go_scatter out_free
 xe_rows xeT_ps xeT hid_ps hid ye_ps yeT yb_ps yout idx0 idx""".split()
ROUNDS = 2


def program(nc, patches, txt, tok_w, tok_b, wq, wk, wv, wfg1, wf2, wg2, wo, norm_w, wr, w1, w2, consts, out):
    with ExitStack() as ctx:
        def sb(name, shape, dt=F32):
            return ctx.enter_context(nc.sbuf_tensor(name, shape, dt))

        sem = {n: ctx.enter_context(nc.semaphore(n)) for n in SEMS}
        sem.update({n: [ctx.enter_context(nc.semaphore(f"{n}{par}")) for par in range(2)] for n in PAIRED})
        psF = ctx.enter_context(nc.psum_tensor("psF", [P, 4, 512], F32))
        psB = ctx.enter_context(nc.psum_tensor("psB", [P, 3, 512], F32))
        psC = ctx.enter_context(nc.psum_tensor("psC", [P, 512], F32))
        table = nc.dram_tensor("table", [E * SLOTS, COLS], F32, kind="Internal").ap()

        cst = sb("cst", [P, CONST_COLS])
        bias = sb("bias", [P, KD])
        wqs, wks, wvs, wos = (sb(n, [P, KD, D]) for n in ("wqs", "wks", "wvs", "wos"))
        won = sb("won", [P, KD, D])
        nw = sb("nw", [P, KD])
        wfg = sb("wfg", [P, KD, 2 * DK])
        wf2s = sb("wf2s", [P, HM])
        wg2s = sb("wg2s", [P, D])
        wrs = sb("wrs", [P, KD, E])
        embT = sb("embT", [P, KD, B * IMG]); img = sb("img", [IMG, B, D])
        w1s = sb("w1s", [P, 2, KD, F]); w2s = sb("w2s", [P, 2, KF, D])
        tokw = w1s[:, :, :, :].rearrange("p a k f -> p (a k f)")[:, 0:KP * D].rearrange("p (k d) -> p k d", k=KP)
        xpat = w2s[:, :, :, :].rearrange("p a k f -> p (a k f)")[:, 0:KP * B * IMG].rearrange(
            "p (k t) -> p k t", k=KP)
        h = sb("h", [R, 2, 2, D])
        st1 = sb("st1", [R, 2, 6]); mv1 = sb("mv1", [R, 2, 2]); ve1 = sb("ve1", [R, 2]); rs1 = sb("rs1", [R, 2])
        xn = sb("xn", [R, 2, D])
        xnT = sb("xnT", [P, KD, 2 * R])
        fgT = sb("fgT", [P, 2 * R])
        qab = sb("qab", [P, 2, 2 * KD * R]); qln = sb("qln", [P, 2, 2 * KD * R])
        kT = sb("kT", [P, KD, 2 * R])
        qB = sb("qB", [P, KD, 4, 2 * R])
        fab = sb("fab", [R, 2, HM]); logf = sb("logf", [P, 2, HM])
        sig = sb("sig", [R, 2, HM]); srow = sb("srow", [R, 2, HM])
        gab = sb("gab", [R, 2 * D]); sg = sb("sg", [R, 2, 2 * D])
        v = sb("v", [P, 2, 2, D])
        eD = sb("eD", [R, 2, 2, HM]); ek = sb("ek", [R, 3, HM])
        S = sb("S", [P, 3, HM])
        ST = sb("ST", [P, 4, 3 * R])
        PT = sb("PT", [P, ROUNDS, 3, 4 * R]); AT = sb("AT", [P, ROUNDS, 3, 4 * R])
        masks = sb("masks", [R, 3, 4 * R])
        u = sb("u", [R, 2, HM]); mx = sb("mx", [R, 2 * H])
        Z = sb("Z", [R, 2 * H]); rZ = sb("rZ", [R, 2 * H])
        rz2 = sb("rz2", [R, 2 * H]); QE = sb("QE", [R, 2, HM]); QET = sb("QET", [P, 4, 2, 2 * R])
        ogn = sb("ogn", [R, 2, D])
        sq = sb("sq", [R, 2, D]); og = sb("og", [R, 2, D]); ss = sb("ss", [R, 6, 2 * H])
        ogT = sb("ogT", [P, KD, 2 * R])
        rows = sb("rows", [R, 2, 2, COLS])
        st2 = sb("st2", [R, 2, 6]); mv2 = sb("mv2", [R, 2, 2]); ve2 = sb("ve2", [R, 2])
        xf = sb("xf", [R, 2, D]); xfT = sb("xfT", [P, KD, 2 * R])
        rt = sb("rt", [R, 12, 2 * E]); rsm = sb("rsm", [R, 8, 2])
        oh = sb("oh", [R, 2, E]); acc = sb("acc", [R, E]); acct = sb("acct", [R, E]); tokc = sb("tokc", [R, 2])
        slot = sb("slot", [R, 2, 2], U32)
        zero = sb("zero", [R, 16 // ZC * COLS])
        er = sb("er", [R, 2, 2, COLS]); res = sb("res", [R, 2, 2, COLS])
        xe = sb("xe", [R, 2, D]); xeT = sb("xeT", [P, KD, SLOTS])
        hid = sb("hid", [P, KF, SLOTS]); yeT = sb("yeT", [P, KD, SLOTS]); yo = sb("yo", [R, 2, 2, D])
        ix0 = sb("ix0", [R, 2, 2]); ix = sb("ix", [R, 2, 2], U32)

        def const(name, rows_=R):
            a, b = CONST[name]
            return cst[0:rows_, a:b]

        def landed(b, par, dmas=1):
            return 8 * dmas * (b - par) + 16 * dmas

        def wait_count(eng, s, count):
            if not isinstance(count, int) or count > 0:
                eng.wait_ge(s, count)

        def flat(x):
            return x.rearrange("p k t -> p (k t)")

        N_WTS = 9
        block = ctx.enter_context(nc.Block())

        @block.sync
        def _(sp):
            def load_text(b, par):
                wait_count(sp, sem["h_kept"], b - 1)
                t = txt[bass.ds(b, 1)].rearrange("o t d -> (o t) d")
                sp.dma_start(h[IMG:R, par, 0, :], t[0:R - IMG]).then_inc(sem["text_in"][par], 16)
                sp.dma_start(h[0:N - R, par, 1, :], t[R - IMG:TXT]).then_inc(sem["text_in"][par], 16)

            def store_h1(b, par):
                sp.wait_ge(sem["h1"], b + 1)
                o = out[bass.ds(b, 1)].rearrange("o t d -> (o t) d")
                sp.dma_start(o[0:R], rows[0:R, par, 0, 0:D]).then_inc(sem["h1_stored"][par], 16)
                sp.dma_start(o[R:N], rows[0:N - R, par, 1, 0:D]).then_inc(sem["h1_stored"][par], 16)
                sp.wait_ge(sem["h1_stored"][par], landed(b, par, 2))
                sp.sem_inc(sem["rows_stored"], 1)

            half = KP // 2
            sp.dma_start(tokw[:, 0:half, :], tok_w[:, 0:half]).then_inc(sem["emb_in"], 16)
            sp.dma_start(tokw[:, half:KP, :], tok_w[:, half:KP]).then_inc(sem["emb_in"], 16)
            sp.dma_start(cst[:, :], consts).then_inc(sem["const_in"], 16)
            sp.wait_ge(sem["zero_set"], 1)
            load_text(0, 0)
            for dst, src in ((wfg[:, :, :], wfg1), (wqs[:, :, :], wq), (wks[:, :, :], wk), (wf2s[0:DK, :], wf2),
                             (wvs[:, :, :], wv), (wg2s[DK:2 * DK, :], wg2), (wos[:, :, :], wo), (nw[:, :], norm_w),
                             (wrs[:, :, :], wr)):
                sp.dma_start(dst, src).then_inc(sem["wts_in"], 16)
            load_text(1, 1)
            for c in range(ZC):
                sp.dma_start(table.rearrange("(c r a) d -> c r (a d)", c=ZC, r=R)[c], zero[:, :]
                             ).then_inc(sem["table_clear"], 16)
            sp.wait_ge(sem["embT_ps"], 1)
            for e in range(2):
                sp.dma_start(w1s[:, e], w1[e]).then_inc(sem["w1_in"][e], 16)
                sp.dma_start(w2s[:, e], w2[e]).then_inc(sem["w2_in"][e], 16)
            sp.sem_inc(sem["rows_stored"], 1)
            with sp.Fori(1, B // 2) as pair:
                i = 2 * pair
                load_text(i, 0)
                store_h1(i - 2, 0)
                load_text(i + 1, 1)
                store_h1(i - 1, 1)
            store_h1(B - 2, 0)
            store_h1(B - 1, 1)

            def table_rows(e):
                t = table.rearrange("(e t r) d -> e r t d", e=E, t=2)[bass.ds(e, 1)]
                return t.rearrange("o r t d -> (o r) t d")

            def load_rows(e, par):
                wait_count(sp, sem["xe_rows"], e - 1)
                sp.dma_start(er[:, par], table_rows(e)).then_inc(sem["rows_in"][par], 16)

            def load_residual(e, par):
                wait_count(sp, sem["yout"], e - 1)
                sp.dma_start(res[:, par], table_rows(e)).then_inc(sem["res_in"][par], 16)

            def load_weights(e, par):
                sp.wait_ge(sem["hid_ps"], 4 * (e - 1))
                sp.dma_start(w1s[:, par], w1[bass.ds(e, 1)].rearrange("o p k f -> (o p) k f")
                             ).then_inc(sem["w1_in"][par], 16)
                sp.wait_ge(sem["ye_ps"], e - 1)
                sp.dma_start(w2s[:, par], w2[bass.ds(e, 1)].rearrange("o p k f -> (o p) k f")
                             ).then_inc(sem["w2_in"][par], 16)

            for par in range(2):
                sp.wait_ge(sem["table_io"][par], 16 * B)
            load_rows(0, 0)
            load_rows(1, 1)
            load_residual(0, 0)
            load_residual(1, 1)
            with sp.Fori(1, E // 2) as pair:
                e = 2 * pair
                load_rows(e, 0)
                load_weights(e, 0)
                load_residual(e, 0)
                load_rows(e + 1, 1)
                load_weights(e + 1, 1)
                load_residual(e + 1, 1)
            for par in range(2):
                sp.wait_ge(sem["out_rows"][par], 16 * E)
                sp.wait_ge(sem["h1_stored"][par], 16 * B)

        @block.tensor
        def _(pe):
            ident = const("ident", P)

            def mm(o, lhsT, rhs, start=True, stop=True):
                return nc.tensor.matmul(o, lhsT, rhs, start=start, stop=stop)

            def embed_all():
                for c in range(KD):
                    for k in range(KP):
                        x = mm(psF[:, c, 0:B * IMG], tokw[:, k, c * P:(c + 1) * P], xpat[:, k, :],
                               k == 0, k == KP - 1)
                x.then_inc(sem["embT_ps"], 1)

            def turn_embeddings():
                for b in range(B):
                    bank, at = [2, 3, 0, 1][b // 2], (b % 2) * D
                    for c in range(KD):
                        x = nc.tensor.transpose(psF[0:IMG, bank, at + c * P:at + (c + 1) * P],
                                                embT[:, c, b * IMG:(b + 1) * IMG], ident)
                    if b % 2:
                        x.then_inc(sem["emb_ps"], 1)

            def turn(o, src, done):
                for t in range(2):
                    for k in range(KD):
                        x = nc.tensor.transpose(o[:, k * 2 * R + t * R:k * 2 * R + (t + 1) * R],
                                                src[:, t, k * P:(k + 1) * P], const("ident")[:, 0:R])
                x.then_inc(done, 1)

            def turn_xn(b):
                pe.wait_ge(sem["xn"], b + 1)
                wait_count(pe, sem["ST"], b)
                turn(psF[:, 1, :], xn, sem["xnT_ps"])

            def project_fg_qk(b):
                pe.wait_ge(sem["xnT"], b + 1)
                for k in range(KD):
                    x = mm(psF[0:2 * DK, 0, 0:2 * R], wfg[:, k, :], xnT[:, k, :], k == 0, k == KD - 1)
                x.then_inc(sem["fg_ps"], 1)
                for w, bank in ((wqs, 2), (wks, 3)):
                    for c in range(KD):
                        for k in range(KD):
                            x = mm(psF[:, bank, c * 2 * R:(c + 1) * 2 * R], w[:, k, c * P:(c + 1) * P],
                                   xnT[:, k, :], k == 0, k == KD - 1)
                x.then_inc(sem["qk_ps"], 1)

            def forget_gates(b):
                pe.wait_ge(sem["fgT"], b + 1)
                for t in range(2):
                    x = mm(psF[0:R, t, :], fgT[:, t * R:(t + 1) * R], wf2s[:, :])
                x.then_inc(sem["f_ps"], 1)

            def values(b):
                pe.wait_ge(sem["qkT"], b + 1)
                for t in range(2):
                    for k in range(KD):
                        x = mm(psF[0:R, 2, t * D:(t + 1) * D], xnT[:, k, t * R:(t + 1) * R], wvs[:, k, :],
                               k == 0, k == KD - 1)
                x.then_inc(sem["v_ps"], 1)

            def gate(b):
                for t in range(2):
                    x = mm(psF[0:R, 3, t * D:(t + 1) * D], fgT[:, t * R:(t + 1) * R], wg2s[:, :])
                x.then_inc(sem["g_ps"], 1)

            def decays(b):
                pe.wait_ge(sem["logf"], b + 1)
                for t in range(2):
                    x = mm(psF[0:R, t, :], const("centre", P), logf[:, t, :])
                x.then_inc(sem["d_ps"], 1)
                pe.wait_ge(sem["v"], b + 1)
                mm(psF[0:R, 2, :], const("cross0", P), logf[:, 0, :], True, False)
                mm(psF[0:R, 2, :], const("cross1", P), logf[:, 1, :], False, True).then_inc(sem["e_ps"], 1)

            def turn_slots(b):
                pe.wait_ge(sem["S_rows"], b + 1)
                pe.wait_ge(sem["eD"], b + 1)
                for hp in range(4):
                    if hp == 3:
                        pe.wait_ge(sem["g_lsg"], b + 1)
                    for a in range(3):
                        x = nc.tensor.transpose(psF[:, hp, a * R:(a + 1) * R], S[0:R, a, hp * P:(hp + 1) * P],
                                                const("ident")[:, 0:R])
                x.then_inc(sem["ST_ps"], 1)

            def qk_products(b, n):
                if n == 0:
                    wait_count(pe, sem["a_kept"], ROUNDS * b)
                    pe.wait_ge(sem["qkT"], b + 1)
                else:
                    pe.wait_ge(sem["p_kept"], ROUNDS * b + n)
                for pair in range(2):
                    mm(psB[0:R, pair, 0:4 * R], kT[:, n, 0:R],
                       qB[:, n, 2 * pair:2 * pair + 2, :].rearrange("p h t -> p (h t)"))
                mm(psB[0:R, 2, 0:4 * R].rearrange("r (h t) -> r h t", h=4), kT[:, n, R:2 * R],
                   qB[:, n, :, R:2 * R]).then_inc(sem["p_ps"], 1)

            def head_weights(w, hh):
                n, pair, two = hh // 4, hh % 4 // 2, hh % 2 * 2 * R
                return (w[:, n, pair, two:two + R], w[:, n, pair, two + R:two + 2 * R],
                        w[:, n, 2, hh % 4 * R:(hh % 4 + 1) * R])

            def slot_scores(b):
                pe.wait_ge(sem["p_kept"], ROUNDS * (b + 1))
                pe.wait_ge(sem["S_rows"], b + 1)
                for hh in range(H):
                    m = slice(hh * M, (hh + 1) * M)
                    own0, cross, own1 = head_weights(PT, hh)
                    mm(psB[0:R, 0, m], own0, S[:, 0, m])
                    mm(psB[0:R, 1, m], cross, S[:, 1, m], True, False)
                    x = mm(psB[0:R, 1, m], own1, S[:, 2, m], False, True)
                x.then_inc(sem["o_ps"], 1)

            def turn_QE(b):
                pe.wait_ge(sem["QE"], b + 1)
                for hp in range(4):
                    for t in range(2):
                        at = (hp % 2) * 2 * R + t * R
                        x = nc.tensor.transpose(psB[:, 1 + hp // 2, at:at + R], QE[:, t, hp * P:(hp + 1) * P],
                                                const("ident")[:, 0:R])
                x.then_inc(sem["QET_ps"], 1)

            def slot_weights(b, n):
                if n == 0:
                    pe.wait_ge(sem["QETa"], b + 1)
                    pe.wait_ge(sem["QETb"], b + 1)
                    pe.wait_ge(sem["ST"], b + 1)
                else:
                    pe.wait_ge(sem["a_kept"], ROUNDS * b + n)
                for pair in range(2):
                    qe, st = QET[:, 2 * n + pair], ST[:, 2 * n + pair, :]
                    both = psB[:, pair, 0:4 * R].rearrange("p (h t) -> p h t", h=2)
                    last = psB[:, 2, 2 * pair * R:2 * (pair + 1) * R].rearrange("p (h t) -> p h t", h=2)
                    mm(both[0:R, :, R:2 * R], st[:, R:2 * R], qe[:, :, R:2 * R])
                    for o, k0, q0 in ((both, 0, 0), (last, 2 * R, R)):
                        mm(o[0:CUT, :, 0:CUT], st[:, k0:k0 + CUT], qe[:, :, q0:q0 + CUT])
                        x = mm(o[0:R, :, CUT:R], st[:, k0:k0 + R], qe[:, :, q0 + CUT:q0 + R])
                x.then_inc(sem["a_ps"], 1)

            def mix_values(b, par):
                wait_count(pe, sem["over"], b)
                wait_count(pe, sem["eslot"], b)
                for hh in range(H):
                    c = slice(hh * DK, (hh + 1) * DK)
                    if hh % 4 == 0:
                        pe.wait_ge(sem["a_kept"], ROUNDS * b + hh // 4 + 1)
                    own0, cross, own1 = head_weights(AT, hh)
                    mm(psC[0:R, c], own0, v[:, par, 0, c])
                    o1 = psC[0:R, D + hh * DK:D + (hh + 1) * DK]
                    mm(o1, cross, v[:, par, 0, c], True, False)
                    x = mm(o1, own1, v[:, par, 1, c], False, True)
                x.then_inc(sem["ov_ps"], 1)

            def turn_output(b):
                pe.wait_ge(sem["og"], b + 1)
                turn(psC, og, sem["ogT_ps"])

            def output_projection(b):
                pe.wait_ge(sem["ogT"], b + 1)
                for t in range(2):
                    for k in range(KD):
                        x = mm(psC[0:R, t * D:(t + 1) * D], ogT[:, k, t * R:(t + 1) * R], won[:, k, :],
                               k == 0, k == KD - 1)
                x.then_inc(sem["wo_ps"], 1)

            def turn_xf(b):
                pe.wait_ge(sem["xf"], b + 1)
                turn(psC, xf, sem["xfT_ps"])

            def logits(b):
                pe.wait_ge(sem["xfT"], b + 1)
                for t in range(2):
                    for k in range(KD):
                        x = mm(psC[0:R, t * E:(t + 1) * E], xfT[:, k, t * R:(t + 1) * R], wrs[:, k, :],
                               k == 0, k == KD - 1)
                x.then_inc(sem["lg_ps"], 1)

            def ranks(b):
                pe.wait_ge(sem["ohv"], b + 1)
                pe.wait_ge(sem["acc2"], b + 1)
                before, ones = const("before"), const("ones")
                r0, r1 = psC[0:R, 2 * E:3 * E], psC[0:R, 3 * E:4 * E]
                mm(r0, before, oh[:, 0, :], True, False)
                mm(r0, ones, acc[:, :], False, True)
                mm(r1, before, oh[:, 1, :], True, False)
                mm(r1, ones, oh[:, 0, :], False, False)
                mm(r1, ones, acc[:, :], False, True).then_inc(sem["rank_ps"], 1)

            def step(i, par, front=True, attend=True, route=True):
                b, bp, c = i - 1, 1 - par, i - 2
                if front:
                    turn_xn(i)
                if attend:
                    qk_products(b, 0)
                if front:
                    project_fg_qk(i)
                if attend:
                    qk_products(b, 1)
                if route:
                    turn_output(c)
                if front:
                    forget_gates(i)
                if route:
                    output_projection(c)
                if attend:
                    slot_scores(b)
                if front:
                    values(i)
                    decays(i)
                    gate(i)
                if route:
                    turn_xf(c)
                if attend:
                    turn_QE(b)
                if route:
                    logits(c)
                if attend:
                    slot_weights(b, 0)
                if front:
                    turn_slots(i)
                if route:
                    ranks(c)
                if attend:
                    slot_weights(b, 1)
                    mix_values(b, bp)

            pe.wait_ge(sem["emb_in"], 16 * 5)
            embed_all()
            pe.wait_ge(sem["const_in"], 16)
            pe.wait_ge(sem["embT"], 1)
            turn_embeddings()
            pe.wait_ge(sem["img_kept"], 4)
            pe.wait_ge(sem["wts_in"], 16 * N_WTS)
            step(0, 0, attend=False, route=False)
            pe.wait_ge(sem["wo_scaled"], 1)
            step(1, 1, route=False)
            with pe.Fori(1, B // 2) as pair:
                i = 2 * pair
                step(i, 0)
                step(i + 1, 1)
            step(B, 0, front=False)
            step(B + 1, 1, front=False, attend=False)

            def turn_inputs(e):
                pe.wait_ge(sem["xe_rows"], e + 1)
                wait_count(pe, sem["xeT"], e)
                turn(psB[:, 0, :], xe, sem["xeT_ps"])

            def hidden(e, par):
                pe.wait_ge(sem["w1_in"][par], landed(e, par))
                pe.wait_ge(sem["xeT"], e + 1)
                for g in range(4):
                    wait_count(pe, sem["hid"], 4 * e + g - 3)
                    for f in range(2):
                        for k in range(KD):
                            c = (2 * g + f) * P
                            x = mm(psF[:, g, f * SLOTS:(f + 1) * SLOTS], w1s[:, par, k, c:c + P], xeT[:, k, :],
                                   k == 0, k == KD - 1)
                    x.then_inc(sem["hid_ps"], 1)

            def outputs(e, par):
                pe.wait_ge(sem["w2_in"][par], landed(e, par))
                pe.wait_ge(sem["hid"], 4 * (e + 1))
                wait_count(pe, sem["yeT"], e)
                for c in range(KD):
                    for k in range(KF):
                        x = mm(psB[:, 1, c * SLOTS:(c + 1) * SLOTS], w2s[:, par, k, c * P:(c + 1) * P], hid[:, k, :],
                               k == 0, k == KF - 1)
                x.then_inc(sem["ye_ps"], 1)

            def turn_outputs(e):
                pe.wait_ge(sem["yeT"], e + 1)
                for t in range(2):
                    for c in range(KD):
                        x = nc.tensor.transpose(psB[0:R, 2, t * D + c * P:t * D + (c + 1) * P],
                                                yeT[:, c, t * R:(t + 1) * R], ident)
                x.then_inc(sem["yb_ps"], 1)

            turn_inputs(0)
            hidden(0, 0)
            turn_inputs(1)
            outputs(0, 0)
            hidden(1, 1)
            with pe.Fori(1, E // 2) as pair:
                for par in range(2):
                    e = 2 * pair + par
                    turn_inputs(e)
                    turn_outputs(e - 2)
                    outputs(e - 1, 1 - par)
                    hidden(e, par)
            pe.wait_ge(sem["yout"], E - 2)
            turn_outputs(E - 2)
            outputs(E - 1, 1)
            pe.wait_ge(sem["yout"], E - 1)
            turn_outputs(E - 1)

        @block.scalar
        def _(act):
            half = KP // 2
            act.dma_start(xpat[:, 0:half, :], patches[:, 0:half]).then_inc(sem["emb_in"], 16)
            act.dma_start(xpat[:, half:KP, :], patches[:, half:KP]).then_inc(sem["emb_in"], 16)
            act.dma_start(bias[:, :], tok_b).then_inc(sem["emb_in"], 16)
            nc.scalar.preload_act_table_set("natural_log_exp_and_others")

            def fn(o, i, f, done, **kw):
                return nc.scalar.activation(o, i, f, **kw).then_inc(done, 1)

            def embedding_bias():
                act.wait_ge(sem["embT_ps"], 1)
                for c in range(KD):
                    x = nc.scalar.activation(embT[:, c, :], psF[:, c, 0:B * IMG], ACT.Identity, bias=bias[:, c:c + 1])
                x.then_inc(sem["embT"], 1)

            def keep_images():
                for n in range(B // 2):
                    act.wait_ge(sem["emb_ps"], n + 1)
                    fn(img[:, 2 * n:2 * n + 2, :].rearrange("r b d -> r (b d)"), psF[0:IMG, [2, 3, 0, 1][n], :], ACT.Copy,
                       sem["img_kept"])

            def head_squares(b):
                act.wait_ge(sem["ogn"], b + 1)
                fn(sq[:, :, :], ogn[:, :, :], ACT.Square, sem["sq"])

            def head_rms(b):
                act.wait_ge(sem["ss3"], b + 1)
                fn(ss[:, 3, :], ss[:, 2, :], ACT.Ln, sem["ss_ln"])
                act.wait_ge(sem["ss_ln"], b + 1)
                fn(ss[:, 4, :], ss[:, 3, :], ACT.Exp, sem["rms"], scale=-0.5)

            def keep(b, dst, src, ready, done):
                act.wait_ge(ready, b + 1)
                fn(dst, src, ACT.Copy, done)

            def sigmoid_qk(b):
                act.wait_ge(sem["qk_ps"], b + 1)
                fn(qab[:, :, :], psF[:, 2:4, 0:4 * R], ACT.Abs, sem["q_abs"])
                act.wait_ge(sem["q_abs"], b + 1)
                fn(qab[:, :, :], qab[:, :, :], ACT.Exp, sem["q_exp"], scale=-1.0)
                act.wait_ge(sem["q_exp"], b + 1)
                fn(qln[:, :, :], qab[:, :, :], ACT.Ln, sem["q_ln"], bias=1.0)

            def sigmoid_f(b):
                act.wait_ge(sem["f_ps"], b + 1)
                fn(fab[:, :, :], psF[0:R, 0:2, :], ACT.Abs, sem["f_abs"])
                act.wait_ge(sem["f_abs"], b + 1)
                fn(fab[:, :, :], fab[:, :, :], ACT.Exp, sem["f_exp"], scale=-1.0)
                act.wait_ge(sem["f_exp"], b + 1)
                fn(fab[:, :, :], fab[:, :, :], ACT.Ln, sem["f_ln"], bias=1.0)

            def qk_sigmoid(b):
                act.wait_ge(sem["q_lsg"], b + 1)
                fn(qab[:, :, :], qln[:, :, :], ACT.Exp, sem["q_sig"])

            def forget(b):
                act.wait_ge(sem["logf"], b + 1)
                wait_count(act, sem["s"], b)
                fn(sig[:, :, :], logf[0:R, :, :], ACT.Exp, sem["f_sig"])

            def sigmoid_gate(b):
                act.wait_ge(sem["g_ps"], b + 1)
                fn(gab[:, :], psF[0:R, 3, :], ACT.Abs, sem["g_abs"])
                act.wait_ge(sem["g_abs"], b + 1)
                fn(gab[:, :], gab[:, :], ACT.Exp, sem["g_exp"], scale=-1.0)
                act.wait_ge(sem["g_exp"], b + 1)
                fn(gab[:, :], gab[:, :], ACT.Ln, sem["g_ln"], bias=1.0)

            def keep_QET(b):
                keep(b, QET[0:M, :, 0, :].rearrange("p (a c) t -> p a c t", a=2),
                     psB[0:M, 1:3, 0:4 * R].rearrange("p a (c t) -> p a c t", c=2), sem["QET_ps"], sem["QETa"])

            def keep_v(b, par):
                wait_count(act, sem["ov_ps"], b - 1)
                keep(b, v[0:R, par].rearrange("r t d -> r (t d)"), psF[0:R, 2, :], sem["v_ps"], sem["v"])

            def decay_keys(b):
                act.wait_ge(sem["d_ps"], b + 1)
                wait_count(act, sem["S_rows"], b)
                fn(ek[:, 0::2, :], psF[0:R, 0:2, :], ACT.Exp, sem["ekD"], scale=-1.0)

            def decay_cross(b):
                act.wait_ge(sem["e_ps"], b + 1)
                fn(ek[:, 1, :], psF[0:R, 2, :], ACT.Exp, sem["ecD"])

            def decay_queries(b, par):
                wait_count(act, sem["QE"], b - 1)
                fn(eD[:, par], psF[0:R, 0:2, :], ACT.Exp, sem["eD"])

            def gate_sigmoid(b, par):
                act.wait_ge(sem["g_lsg"], b + 1)
                wait_count(act, sem["ogn"], b - 1)
                fn(sg[:, par], gab[:, :], ACT.Exp, sem["g_sig"])

            def numerators(b):
                act.wait_ge(sem["umx"], b + 1)
                fn(u[:, :, :], u[:, :, :], ACT.Exp, sem["pexp"])

            def logit_exps(b):
                act.wait_ge(sem["ldm"], b + 1)
                fn(rt[:, 1, :], rt[:, 0, :], ACT.Exp, sem["lexp"])

            def step(i, par, front=True, attend=True, route=True):
                b, bp, c = i - 1, 1 - par, i - 2
                if front:
                    keep(i, flat(xnT[:, :, :]), psF[:, 1, 0:4 * R], sem["xnT_ps"], sem["xnT"])
                if route:
                    head_squares(c)
                    head_rms(c)
                if front:
                    sigmoid_qk(i)
                if route:
                    keep(c, flat(ogT[:, :, :]), psC[:, 0:4 * R], sem["ogT_ps"], sem["ogT"])
                if front:
                    qk_sigmoid(i)
                    sigmoid_f(i)
                    forget(i)
                    keep_v(i, par)
                    decay_keys(i)
                if attend:
                    numerators(b)
                if front:
                    decay_cross(i)
                    decay_queries(i, par)
                if route:
                    keep(c, flat(xfT[:, :, :]), psC[:, 0:4 * R], sem["xfT_ps"], sem["xfT"])
                if attend:
                    keep_QET(b)
                if front:
                    sigmoid_gate(i)
                if route:
                    logit_exps(c)
                if front:
                    gate_sigmoid(i, par)

            act.wait_ge(sem["emb_in"], 16 * 5)
            embedding_bias()
            keep_images()
            step(0, 0, attend=False, route=False)
            step(1, 1, route=False)
            with act.Fori(1, B // 2) as pair:
                i = 2 * pair
                step(i, 0)
                step(i + 1, 1)
            step(B, 0, front=False)
            step(B + 1, 1, front=False, attend=False)

            def keep_inputs(e):
                keep(e, flat(xeT[:, :, :]), psB[:, 0, 0:4 * R], sem["xeT_ps"], sem["xeT"])

            def keep_outputs(e):
                keep(e, flat(yeT[:, :, :]), psB[:, 1, 0:4 * R], sem["ye_ps"], sem["yeT"])

            def relu(e):
                for g in range(4):
                    act.wait_ge(sem["hid_ps"], 4 * e + g + 1)
                    fn(flat(hid[:, 2 * g:2 * g + 2, :]), psF[:, g, 0:4 * R], ACT.Relu, sem["hid"])

            keep_inputs(0)
            relu(0)
            keep_inputs(1)
            keep_outputs(0)
            relu(1)
            with act.Fori(1, E // 2) as pair:
                for par in range(2):
                    e = 2 * pair + par
                    keep_inputs(e)
                    act.wait_ge(sem["yb_ps"], e - 1)
                    keep_outputs(e - 1)
                    relu(e)
            act.wait_ge(sem["yb_ps"], E - 1)
            keep_outputs(E - 1)

        @block.vector
        def _(dve):
            def tt(o, a, b_, op, done):
                return nc.vector.tensor_tensor(o, a, b_, op).then_inc(done, 1)

            def apart():
                dve.wait_ge(sem["const_in"], 16)

            def hidden_stats(b, par):
                dve.wait_ge(sem["img_kept"], 4)
                wait_count(dve, sem["h_kept"], b - 1)
                nc.vector.tensor_copy(h[0:IMG, par, 0, :], img[:, bass.ds(b, 1), :].rearrange("r o d -> r (o d)")
                                      ).then_inc(sem["h_img"], 1)
                dve.wait_ge(sem["text_in"][par], landed(b, par, 2))
                dve.wait_ge(sem["h_img"], b + 1)
                for t in range(2):
                    x = nc.vector.bn_stats(st1[:, t, :], h[:, par, t, :])
                x.then_inc(sem["stats1"], 1)
                apart()
                dve.wait_ge(sem["stats1"], b + 1)
                for t in range(2):
                    x = nc.vector.bn_aggr(mv1[:, t, :], st1[:, t, :])
                x.then_inc(sem["mv1"], 1)

            def layernorm1(b, par):
                dve.wait_ge(sem["rstd1"], b + 1)
                wait_count(dve, sem["xnT_ps"], b)
                for t in range(2):
                    x = nc.vector.tensor_scalar(xn[:, t, :], h[:, par, t, :], mv1[:, t, 0:1], rs1[:, t:t + 1],
                                                ALU.subtract, ALU.mult)
                x.then_inc(sem["xn"], 1)

            def keep_fg(b):
                dve.wait_ge(sem["fg_ps"], b + 1)
                nc.vector.tensor_copy(fgT[0:2 * DK, :], psF[0:2 * DK, 0, 0:2 * R]).then_inc(sem["fgT"], 1)

            def log_sigmoid_qk(b):
                dve.wait_ge(sem["q_ln"], b + 1)
                nc.vector.scalar_tensor_tensor(out=qln[:, :, :], in0=psF[:, 2:4, 0:4 * R], scalar=0.0,
                                               in1=qln[:, :, :], op0=ALU.min, op1=ALU.subtract
                                               ).then_inc(sem["q_lsg"], 1)

            def log_forget(b):
                dve.wait_ge(sem["f_ln"], b + 1)
                wait_count(dve, sem["e_ps"], b)
                wait_count(dve, sem["f_sig"], b)
                nc.vector.scalar_tensor_tensor(out=logf[0:R, :, :], in0=psF[0:R, 0:2, :], scalar=0.0,
                                               in1=fab[:, :, :], op0=ALU.min, op1=ALU.subtract
                                               ).then_inc(sem["logf"], 1)

            def silu_qk(b):
                dve.wait_ge(sem["q_sig"], b + 1)
                wait_count(dve, sem["p_ps"], ROUNDS * b)
                nc.vector.tensor_tensor(flat(kT[:, :, :]), psF[:, 3, 0:4 * R], qab[:, 1, :], ALU.mult)
                for g in range(4):
                    ps = slice(g * DK, (g + 1) * DK)
                    x = nc.vector.tensor_tensor(qB[ps, :, g, :], psF[ps, 2, 0:4 * R].rearrange("p (k t) -> p k t", k=KD),
                                                qab[ps, 0, :].rearrange("p (k t) -> p k t", k=KD), ALU.mult)
                x.then_inc(sem["qkT"], 1)

            def log_gate(b):
                dve.wait_ge(sem["g_ln"], b + 1)
                nc.vector.scalar_tensor_tensor(out=gab[:, :], in0=psF[0:R, 3, :], scalar=0.0, in1=gab[:, :],
                                               op0=ALU.min, op1=ALU.subtract).then_inc(sem["g_lsg"], 1)

            def keep_ST(b):
                dve.wait_ge(sem["ST_ps"], b + 1)
                wait_count(dve, sem["a_ps"], ROUNDS * b)
                nc.vector.tensor_copy(ST[:, :, :], psF[:, 0:4, 0:3 * R]).then_inc(sem["ST"], 1)

            def keep_QET(b):
                dve.wait_ge(sem["QET_ps"], b + 1)
                nc.vector.tensor_copy(QET[M:P, :, 1, :].rearrange("p (a c) t -> p a c t", a=2),
                                      psB[M:P, 1:3, 0:4 * R].rearrange("p a (c t) -> p a c t", c=2)
                                      ).then_inc(sem["QETb"], 1)

            def mask_P(b, n):
                dve.wait_ge(sem["p_ps"], ROUNDS * b + n + 1)
                tt(PT[0:R, n], psB[0:R, 0:3, 0:4 * R], masks[:, :, :], ALU.mult, sem["p_kept"])

            def mask_A(b, n):
                dve.wait_ge(sem["a_ps"], ROUNDS * b + n + 1)
                nc.vector.scalar_tensor_tensor(
                    out=AT[0:R, n], in0=psB[0:R, 0:3, 0:4 * R], scalar=ABIG,
                    in1=masks[:, :, :], op0=ALU.min, op1=ALU.mult).then_inc(sem["a_kept"], 1)

            def slots(x):
                return x[:, :, :].rearrange("r t (h m) -> r (t h) m", m=M)

            def softmax_shift(b, par):
                dve.wait_ge(sem["o_ps"], b + 1)
                tt(u[:, :, :], psB[0:R, 0:2, :], eD[:, par], ALU.mult, sem["u"])
                dve.wait_ge(sem["u"], b + 1)
                nc.vector.tensor_reduce(mx[:, :], slots(u), AX_X, ALU.max).then_inc(sem["umax"], 1)
                dve.wait_ge(sem["umax"], b + 1)
                tt(slots(u), slots(u), mx[:, :].unsqueeze(2).to_broadcast([R, 2 * H, M]), ALU.subtract, sem["umx"])

            def scale_queries(b, par):
                dve.wait_ge(sem["pexp"], b + 1)
                wait_count(dve, sem["QET_ps"], b)
                tt(QE[:, :, :], u[:, :, :], eD[:, par], ALU.mult, sem["QE"])

            def denominators(b):
                nc.vector.tensor_reduce(Z[:, :], slots(u), AX_X, ALU.add).then_inc(sem["Z"], 1)
                dve.wait_ge(sem["Z"], b + 1)
                wait_count(dve, sem["scale"], b)
                nc.vector.reciprocal(rZ[:, :], Z[:, :]).then_inc(sem["rZ"], 1)
                dve.wait_ge(sem["rZ"], b + 1)
                tt(rz2[:, :], rZ[:, :], rZ[:, :], ALU.mult, sem["rz2"])

            def gate_output(b, par):
                dve.wait_ge(sem["ov_ps"], b + 1)
                dve.wait_ge(sem["g_sig"], b + 1)
                wait_count(dve, sem["og"], b)
                tt(ogn[:, :, :].rearrange("r t d -> r (t d)"), psC[0:R, :], sg[:, par], ALU.mult, sem["ogn"])

            def head_means(b):
                dve.wait_ge(sem["sq"], b + 1)
                nc.vector.tensor_reduce(ss[:, 0, :], sq[:, :, :].rearrange("r t (h c) -> r (t h) c", c=DK), AX_X,
                                        ALU.add).then_inc(sem["ss"], 1)
                dve.wait_ge(sem["ss"], b + 1)
                dve.wait_ge(sem["rz2"], b + 1)
                tt(ss[:, 1, :], ss[:, 0, :], rz2[:, :], ALU.mult, sem["ss2"])
                dve.wait_ge(sem["ss2"], b + 1)
                nc.vector.tensor_scalar(ss[:, 2, :], ss[:, 1, :], 1.0 / DK, RMS_EPS, ALU.mult, ALU.add
                                        ).then_inc(sem["ss3"], 1)

            def residual_stats(b, par):
                dve.wait_ge(sem["wo_ps"], b + 1)
                dve.wait_ge(sem["h_kept"], b + 1)
                tt(rows[:, par, :, 0:D], psC[0:R, :].rearrange("r (t d) -> r t d", t=2), rows[:, par, :, 0:D],
                   ALU.add, sem["h1"])
                dve.wait_ge(sem["h1"], b + 1)
                for t in range(2):
                    x = nc.vector.bn_stats(st2[:, t, :], rows[:, par, t, 0:D])
                x.then_inc(sem["stats2"], 1)
                apart()
                dve.wait_ge(sem["stats2"], b + 1)
                for t in range(2):
                    x = nc.vector.bn_aggr(mv2[:, t, :], st2[:, t, :])
                x.then_inc(sem["mv2"], 1)

            def layernorm2(b, par):
                dve.wait_ge(sem["rstd2"], b + 1)
                nc.vector.scalar_tensor_tensor(out=rows[:, par, :, C_NMR], in0=mv2[:, :, 0], scalar=-1.0,
                                               in1=rows[:, par, :, C_RSTD], op0=ALU.mult, op1=ALU.mult
                                               ).then_inc(sem["nmr"], 1)
                dve.wait_ge(sem["nmr"], b + 1)
                for t in range(2):
                    x = nc.vector.tensor_scalar(xf[:, t, :], rows[:, par, t, 0:D], rows[:, par, t, C_RSTD:C_RSTD + 1],
                                                rows[:, par, t, C_NMR:C_NMR + 1], ALU.mult, ALU.add)
                x.then_inc(sem["xf"], 1)
                nc.vector.tensor_copy(rows[:, par, :, C_TOK], tokc[:, :]).then_inc(sem["tokset"], 1)
                dve.wait_ge(sem["tokset"], b + 1)
                nc.vector.tensor_scalar(tokc[:, :], tokc[:, :], float(N), None, ALU.add).then_inc(sem["toknext"], 1)

            def e3(x):
                return x.rearrange("r (t e) -> r t e", e=E)

            def choose_expert(b, par):
                def bc(x):
                    return x.unsqueeze(2).to_broadcast([R, 2, E])
                dve.wait_ge(sem["lg_ps"], b + 1)
                nc.vector.tensor_reduce(rsm[:, 0, :], e3(psC[0:R, 0:2 * E]), AX_X, ALU.max
                                        ).then_inc(sem["lmax"], 1)
                dve.wait_ge(sem["lmax"], b + 1)
                tt(e3(rt[:, 0, :]), e3(psC[0:R, 0:2 * E]), bc(rsm[:, 0, :]), ALU.subtract, sem["ldm"])
                dve.wait_ge(sem["ldm"], b + 1)
                nc.vector.scalar_tensor_tensor(out=rt[:, 2, :], in0=rt[:, 0, :], scalar=0.0, in1=const("rev"),
                                               op0=ALU.is_ge, op1=ALU.mult).then_inc(sem["pick"], 1)
                dve.wait_ge(sem["pick"], b + 1)
                nc.vector.tensor_reduce(rsm[:, 1, :], e3(rt[:, 2, :]), AX_X, ALU.max).then_inc(sem["pickmax"], 1)
                dve.wait_ge(sem["pickmax"], b + 1)
                tt(e3(rt[:, 3, :]), e3(const("rev")), bc(rsm[:, 1, :]), ALU.is_equal, sem["oh"])
                dve.wait_ge(sem["oh"], b + 1)
                dve.wait_ge(sem["acc2"], b + 1)
                tt(oh[:, :, :], e3(rt[:, 3, :]), e3(const("validE")), ALU.mult, sem["ohv"])

            def probability(b, par):
                dve.wait_ge(sem["lexp"], b + 1)
                nc.vector.tensor_reduce(rsm[:, 2, :], e3(rt[:, 1, :]), AX_X, ALU.add).then_inc(sem["lsum"], 1)
                dve.wait_ge(sem["lsum"], b + 1)
                nc.vector.reciprocal(rows[:, par, :, C_PROB], rsm[:, 2, :]).then_inc(sem["prob"], 1)

            def choose_slot(b, par):
                dve.wait_ge(sem["rank_ps"], b + 1)
                rank = psC[0:R, 2 * E:4 * E]
                nc.vector.tensor_scalar(rt[:, 4, :], rank, float(CAP), FAR, ALU.is_ge, ALU.mult
                                        ).then_inc(sem["over"], 1)
                tt(rt[:, 5, :], rank, const("ebase"), ALU.add, sem["eslot"])
                dve.wait_ge(sem["over"], b + 1)
                dve.wait_ge(sem["eslot"], b + 1)
                tt(rt[:, 6, :], rt[:, 4, :], rt[:, 5, :], ALU.add, sem["slotx"])
                dve.wait_ge(sem["slotx"], b + 1)
                dve.wait_ge(sem["ohv"], b + 1)
                tt(rt[:, 7, :], rt[:, 6, :], oh[:, :, :].rearrange("r t e -> r (t e)"), ALU.mult, sem["slotoh"])
                tt(acct[:, :], oh[:, 0, :], oh[:, 1, :], ALU.add, sem["acc1"])
                dve.wait_ge(sem["slotoh"], b + 1)
                nc.vector.tensor_reduce(rsm[:, 3, :], e3(rt[:, 7, :]), AX_X, ALU.add).then_inc(sem["slotsum"], 1)
                dve.wait_ge(sem["acc1"], b + 1)
                tt(acc[:, :], acc[:, :], acct[:, :], ALU.add, sem["acc2"])
                dve.wait_ge(sem["slotsum"], b + 1)
                tt(slot[:, par, :], rsm[:, 3, :], const("far"), ALU.add, sem["slot"])

            def step(i, par, front=True, attend=True, route=True):
                b, bp, c = i - 1, 1 - par, i - 2
                if front:
                    hidden_stats(i, par)
                if route:
                    denominators(c)
                if front:
                    layernorm1(i, par)
                if route:
                    gate_output(c, par)
                    head_means(c)
                if attend:
                    mask_P(b, 0)
                if front:
                    keep_fg(i)
                if attend:
                    mask_P(b, 1)
                if front:
                    log_sigmoid_qk(i)
                    silu_qk(i)
                if route:
                    residual_stats(c, par)
                if front:
                    log_forget(i)
                if attend:
                    softmax_shift(b, bp)
                if route:
                    layernorm2(c, par)
                if attend:
                    scale_queries(b, bp)
                    keep_QET(b)
                if route:
                    choose_expert(c, par)
                if front:
                    log_gate(i)
                if attend:
                    mask_A(b, 0)
                if front:
                    keep_ST(i)
                if route:
                    probability(c, par)
                    choose_slot(c, par)
                if attend:
                    mask_A(b, 1)

            nc.vector.memset(h[64:R, :, 1, :], 0.0)
            nc.vector.memset(acc[:, :], 0.0).then_inc(sem["acc2"], 1)
            for x in (wf2s[:, :], wg2s[:, :], fgT[2 * DK:P, :], qB[:, :, :, :], logf[64:P, :, :], v[64:P],
                      S[64:P, :, :], PT[64:P], AT[64:P], QET[:, :, :, :]):
                nc.vector.memset(x, 0.0)
            nc.vector.memset(zero[:, :], 0.0).then_inc(sem["zero_set"], 1)
            dve.wait_ge(sem["const_in"], 16)
            tri, causal = const("mask")[:, 0:R], const("mask")
            for bank in range(2):
                nc.vector.tensor_copy(masks[:, bank, :].rearrange("r (h t) -> r h t", h=2),
                                      causal.unsqueeze(1).to_broadcast([R, 2, 2 * R]))
            nc.vector.tensor_copy(masks[:, 2, :].rearrange("r (h t) -> r h t", h=4),
                                  tri.unsqueeze(1).to_broadcast([R, 4, R]))
            nc.vector.tensor_copy(tokc[:, :], const("tok")).then_inc(sem["zero_set"], 1)
            dve.wait_ge(sem["zero_set"], 2)
            step(0, 0, attend=False, route=False)
            dve.wait_ge(sem["wts_in"], 16 * N_WTS)
            for k in range(KD):
                x = nc.vector.tensor_scalar(won[:, k, :], wos[:, k, :], nw[:, k:k + 1], None, ALU.mult)
            x.then_inc(sem["wo_scaled"], 1)
            step(1, 1, route=False)
            with dve.Fori(1, B // 2) as pair:
                i = 2 * pair
                step(i, 0)
                step(i + 1, 1)
            step(B, 0, front=False)
            step(B + 1, 1, front=False, attend=False)

            def expert_inputs(e, par):
                dve.wait_ge(sem["rows_in"][par], landed(e, par))
                wait_count(dve, sem["xeT_ps"], e)
                for t in range(2):
                    x = nc.vector.tensor_scalar(xe[:, t, :], er[:, par, t, 0:D], er[:, par, t, C_RSTD:C_RSTD + 1],
                                                er[:, par, t, C_NMR:C_NMR + 1], ALU.mult, ALU.add)
                x.then_inc(sem["xe_rows"], 1)

            def expert_outputs(e, par):
                dve.wait_ge(sem["res_in"][par], landed(e, par))
                dve.wait_ge(sem["out_free"], e + 1)
                nc.vector.tensor_scalar(ix0[:, par, :], res[:, par, :, C_TOK], 0.0, FAR + 1.0, ALU.is_equal, ALU.mult
                                        ).then_inc(sem["idx0"], 1)
                dve.wait_ge(sem["idx0"], e + 1)
                nc.vector.scalar_tensor_tensor(out=ix[:, par, :], in0=res[:, par, :, C_TOK], scalar=-1.0,
                                               in1=ix0[:, par, :], op0=ALU.add, op1=ALU.add).then_inc(sem["idx"], 1)
                dve.wait_ge(sem["yb_ps"], e + 1)
                for t in range(2):
                    x = nc.vector.scalar_tensor_tensor(out=yo[:, par, t, :], in0=psB[0:R, 2, t * D:(t + 1) * D],
                                                       scalar=res[:, par, t, C_PROB:C_PROB + 1],
                                                       in1=res[:, par, t, 0:D], op0=ALU.mult, op1=ALU.add)
                x.then_inc(sem["yout"], 1)

            expert_inputs(0, 0)
            expert_inputs(1, 1)
            with dve.Fori(1, E // 2) as pair:
                for par in range(2):
                    expert_inputs(2 * pair + par, par)
                    expert_outputs(2 * pair + par - 2, par)
            expert_outputs(E - 2, 0)
            expert_outputs(E - 1, 1)

        @block.gpsimd
        def _(pool):
            def rstd(b, mv, ve, o, ready, mid, done):
                pool.wait_ge(ready, b + 1)
                nc.gpsimd.tensor_tensor(ve[:, :], mv[:, :, 1], const("lneps"), ALU.add).then_inc(mid, 1)
                pool.wait_ge(mid, b + 1)
                nc.gpsimd.tensor_tensor(o, ve[:, :], const("neghalf"), ALU.pow).then_inc(done, 1)

            def keep_h(b, par):
                pool.wait_ge(sem["h_img"], b + 1)
                pool.wait_ge(sem["text_in"][par], landed(b, par, 2))
                wait_count(pool, sem["rows_stored"], b)
                nc.gpsimd.tensor_tensor(rows[:, par, :, 0:D], h[:, par],
                                        const("zero").unsqueeze(1).to_broadcast([R, 2, D]), ALU.add
                                        ).then_inc(sem["h_kept"], 1)

            def slot_values(b):
                pool.wait_ge(sem["f_sig"], b + 1)
                nc.gpsimd.tensor_tensor(srow[:, :, :], const("ones")[:, 0:1].unsqueeze(1).to_broadcast([R, 2, HM]),
                                        sig[:, :, :], ALU.subtract).then_inc(sem["s"], 1)

            def scale_slots(b):
                pool.wait_ge(sem["ekD"], b + 1)
                pool.wait_ge(sem["s"], b + 1)
                wait_count(pool, sem["o_ps"], b)
                wait_count(pool, sem["ST_ps"], b)
                nc.gpsimd.tensor_tensor(S[0:R, 0::2, :], srow[:, :, :], ek[:, 0::2, :], ALU.mult)
                pool.wait_ge(sem["ecD"], b + 1)
                nc.gpsimd.tensor_tensor(S[0:R, 1, :], srow[:, 0, :], ek[:, 1, :], ALU.mult
                                        ).then_inc(sem["S_rows"], 1)

            def normalise(b):
                pool.wait_ge(sem["rms"], b + 1)
                pool.wait_ge(sem["rZ"], b + 1)
                nc.gpsimd.tensor_tensor(ss[:, 5, :], ss[:, 4, :], rZ[:, :], ALU.mult).then_inc(sem["scale"], 1)
                pool.wait_ge(sem["scale"], b + 1)
                pool.wait_ge(sem["ogn"], b + 1)
                nc.gpsimd.tensor_tensor(og[:, :, :].rearrange("r t (h c) -> r (t h) c", c=DK),
                                        ogn[:, :, :].rearrange("r t (h c) -> r (t h) c", c=DK),
                                        ss[:, 5, :].unsqueeze(2).to_broadcast([R, 2 * H, DK]), ALU.mult
                                        ).then_inc(sem["og"], 1)

            def dispatch(b, par):
                pool.wait_ge(sem["slot"], b + 1)
                pool.wait_ge(sem["prob"], b + 1)
                pool.wait_ge(sem["tokset"], b + 1)
                pool.sem_inc(sem["go_dispatch"], 1)
                for t in range(2):
                    nc.gpsimd.indirect_dma_start(
                        out=table, out_offset=bass.IndirectOffsetOnAxis(ap=slot[:, par, t:t + 1], axis=0),
                        in_=rows[:, par, t, :], in_offset=None, bounds_check=E * SLOTS - 1, oob_is_err=False
                        ).then_inc(sem["table_io"][par], 16)

            def step(i, par, front=True, attend=True, route=True):
                b, bp, c = i - 1, 1 - par, i - 2
                if front:
                    rstd(i, mv1, ve1, rs1[:, :], sem["mv1"], sem["ve1"], sem["rstd1"])
                if route:
                    normalise(c)
                if attend:
                    keep_h(b, bp)
                if route:
                    rstd(c, mv2, ve2, rows[:, par, :, C_RSTD], sem["mv2"], sem["ve2"], sem["rstd2"])
                if front:
                    slot_values(i)
                    scale_slots(i)
                if route:
                    dispatch(c, par)
                    pool.wait_ge(sem["table_io"][par], landed(c, par, 2))

            pool.wait_ge(sem["const_in"], 16)
            pool.wait_ge(sem["zero_set"], 1)
            step(0, 0, attend=False, route=False)
            step(1, 1, route=False)
            pool.wait_ge(sem["table_clear"], 16 * ZC)
            with pool.Fori(1, B // 2) as pair:
                i = 2 * pair
                step(i, 0)
                step(i + 1, 1)
            step(B, 0, front=False)
            step(B + 1, 1, front=False, attend=False)

            out_rows = out.rearrange("b n d -> (b n) d")

            def scatter(e, par):
                pool.wait_ge(sem["yout"], e + 1)
                pool.wait_ge(sem["idx"], e + 1)
                pool.sem_inc(sem["go_scatter"], 1)
                for t in range(2):
                    nc.gpsimd.indirect_dma_start(
                        out=out_rows, out_offset=bass.IndirectOffsetOnAxis(ap=ix[:, par, t:t + 1], axis=0),
                        in_=yo[:, par, t, :], in_offset=None, bounds_check=B * N - 1, oob_is_err=False
                        ).then_inc(sem["out_rows"][par], 16)
                if not isinstance(e, int) or e > 0:
                    pool.wait_ge(sem["out_rows"][1 - par], landed(e - 1, 1 - par, 2))
                    pool.sem_inc(sem["out_free"], 1)

            pool.sem_inc(sem["out_free"], 2)
            for par in range(2):
                pool.wait_ge(sem["h1_stored"][par], 16 * B)
            scatter(0, 0)
            scatter(1, 1)
            with pool.Fori(1, E // 2) as pair:
                scatter(2 * pair, 0)
                scatter(2 * pair + 1, 1)


def shape_constants():
    c = np.zeros((P, CONST_COLS), np.float32)

    def put(name, a):
        lo, hi = CONST[name]
        c[:a.shape[0], lo:hi] = a

    i, t = np.arange(R)[:, None], np.arange(R)[None, :]
    tri = (i <= t)
    put("ident", np.eye(P))
    put("mask", np.concatenate([tri, np.ones((R, R))], 1))
    put("centre", (i <= t).astype(np.float32) - (i <= MID))
    put("cross0", i > t)
    put("cross1", np.broadcast_to(i <= MID, (R, R)))
    put("before", i < t)
    put("ones", np.ones((R, R)))
    put("rev", np.tile(E - np.arange(E), (R, 2)))
    put("ebase", np.tile(SLOTS * np.arange(E), (R, 2)))
    real = np.ones((R, 2)); real[R - 1, 1] = 0
    put("valid", real)
    put("validE", np.repeat(real, E, axis=1))
    put("far", (1 - real) * FAR)
    put("tok", np.arange(R)[:, None] + np.array([[1, R + 1]]))
    put("neghalf", np.full((R, 2), -0.5))
    put("lneps", np.full((R, 2), LN_EPS))
    return c


def kernel(**inputs):
    import concourse.bacc as bacc
    from concourse.bass_utils import run_bass_kernel_spmd

    a = {k: np.asarray(x) for k, x in inputs.items()}

    def tiles(w):
        return w.reshape(-1, P, w.shape[-1]).transpose(1, 0, 2)

    patches = a["x"].reshape(B, 3, 7, PATCH, 7, PATCH).transpose(0, 2, 4, 1, 3, 5).reshape(B, IMG, KP, P)
    laid = {
        "patches": patches.transpose(3, 2, 0, 1).reshape(P, KP, B * IMG),
        "txt": a["txt"],
        "tok_w": tiles(a["L0_tok_W"].T),
        "tok_b": a["L0_tok_b"].reshape(KD, P).T,
        "wq": tiles(a["L0_attn_Wq"]), "wk": tiles(a["L0_attn_Wk"]), "wv": tiles(a["L0_attn_Wv"]),
        "wfg1": tiles(np.concatenate([a["L0_attn_Wf1"], a["L0_attn_Wg1"]], 1)),
        "wf2": a["L0_attn_Wf2"], "wg2": a["L0_attn_Wg2"], "wo": tiles(a["L0_attn_Wo"]),
        "norm_w": a["L0_attn_norm_w"].reshape(KD, P).T,
        "wr": tiles(a["L0_ffn_Wr"]),
        "w1": a["L0_ffn_W1"].reshape(E, KD, P, F).transpose(0, 2, 1, 3),
        "w2": a["L0_ffn_W2"].reshape(E, KF, P, D).transpose(0, 2, 1, 3),
        "consts": shape_constants(),
    }
    nc = bacc.Bacc("TRN2", target_bir_lowering=False, num_devices=1)
    arrays, args = {}, []
    for name, x in laid.items():
        x = np.ascontiguousarray(x)
        arrays["in_" + name] = x
        args.append(nc.dram_tensor("in_" + name, x.shape, mybir.dt.from_np(x.dtype), kind="ExternalInput").ap())
    args.append(nc.dram_tensor("out", (B, N, D), F32, kind="ExternalOutput").ap())
    program(nc, *args)
    r = run_bass_kernel_spmd(nc, [arrays], core_ids=[0])
    return r.results[0]["out"]
```

```python
from contextlib import ExitStack

import numpy as np
import concourse.bass as bass
from concourse import mybir

ALU = mybir.AluOpType
ACT = mybir.ActivationFunctionType
F32 = mybir.dt.float32
U32 = mybir.dt.uint32
F32R = mybir.dt.float32r
AX_X = mybir.AxisListType.X

P = 128
B = 8
IMG = 49
TXT = 128
N = IMG + TXT
R = (N + 1) // 2
PATCH = 16
PD = 3 * PATCH * PATCH
KP = PD // P
D = 256
KD = D // P
H, M, DK = 8, 64, 32
HM = H * M
F = 1024
KF = F // P
E = 8
CAP = B * N // E
SLOTS = 2 * R
MID = R // 2
CUT = 64
LN_EPS = 1e-5
RMS_EPS = 1e-5
FAR = 8192.0
ZC = 8
COLS = D + 4
C_NMR, C_RSTD, C_TOK, C_PROB = D, D + 1, D + 2, D + 3
ABIG = 1e30

CONST = {}
_at = 0
for _name, _w in (("ident", P), ("mask", 2 * R), ("centre", R), ("cross0", R), ("cross1", R), ("before", R),
                  ("ones", R), ("rev", 2 * E), ("full", 2 * E), ("first", E), ("far", 2), ("tok", 2), ("rowlen", 2),
                  ("heads", 4), ("lneps", 1), ("zero", D), ("validE", 2 * E)):
    CONST[_name] = (_at, _at + _w)
    _at += _w
CONST_COLS = _at

PAIRED = "emb_in text_in table_io h1_stored out_rows w1_in w2_in rows_in res_in".split()
SEMS = """const_in wts_in table_clear zero_set rows_stored embT_ps embT img_kept
 emb_ps h_img stats1 mv1 ln1 rstd1 xn xnT_ps xnT fg_ps fgT qk_ps f_ps v_ps g_ps
 q_exp q_ln q_sig qkT f_exp f_ln nl_hi nl_lo f_sig s g_exp g_ln g_sig v
 d_ps e_ps eD ekD ecD S_rows ST_ps ST h_kept
 p_ps p_kept o_ps u umax umx pexp Z rZ rz2 QE QET_ps QETa QETb a_ps a_kept ov_ps ogn
 sq ss_ps ss2 ss3 ss_ln rms scale scale_ps ogT wo_ps h1 stats2 mv2 ln2 rstd2 nmr xf xfT_ps xfT
 lg_ps lmax ldm lexp lsum prob pick pickmax oh ohv rank_ps over slotx slotoh slotsum slot acc1 acc2
 tokset toknext wo_scaled go_dispatch go_scatter out_free
 xe_rows xeT_ps xeT hid_ps hid ye_ps yeT yb_ps yout idx0 idx""".split()
ROUNDS = 2


def program(nc, patches, txt, tok_w, tok_b, wq, wk, wv, wfg1, wf2, wg2, wo, norm_w, wr, w1, w2, consts, out):
    with ExitStack() as ctx:
        def sb(name, shape, dt=F32):
            return ctx.enter_context(nc.sbuf_tensor(name, shape, dt))

        sem = {n: ctx.enter_context(nc.semaphore(n)) for n in SEMS}
        sem.update({n: [ctx.enter_context(nc.semaphore(f"{n}{par}")) for par in range(2)] for n in PAIRED})
        psF = ctx.enter_context(nc.psum_tensor("psF", [P, 4, 512], F32))
        psB = ctx.enter_context(nc.psum_tensor("psB", [P, 3, 512], F32))
        psC = ctx.enter_context(nc.psum_tensor("psC", [P, 512], F32))
        lgs, ranked = psF[0:R, 3, 0:2 * E], psF[0:R, 3, 2 * E:4 * E]
        table = nc.dram_tensor("table", [E * SLOTS, COLS], F32, kind="Internal").ap()

        cst = sb("cst", [P, CONST_COLS])
        bias = sb("bias", [P, KD])
        wqs, wks, wvs, wos = (sb(n, [P, KD, D]) for n in ("wqs", "wks", "wvs", "wos"))
        won = sb("won", [P, KD, D])
        nw = sb("nw", [P, KD])
        wfg = sb("wfg", [P, KD, 2 * DK])
        wf2s = sb("wf2s", [P, HM])
        wg2s = sb("wg2s", [P, D])
        wrs = sb("wrs", [P, KD, E])
        embT = sb("embT", [P, KD, B * IMG]); img = sb("img", [IMG, B, D])
        w1s = sb("w1s", [P, 2, KD, F]); w2s = sb("w2s", [P, 2, KF, D])
        tokw = w1s[:, :, :, :].rearrange("p a k f -> p (a k f)")[:, 0:KP * D].rearrange("p (k d) -> p k d", k=KP)
        xpat = w2s[:, :, :, :].rearrange("p a k f -> p (a k f)")[:, 0:KP * B * IMG].rearrange(
            "p (k t) -> p k t", k=KP)
        h = sb("h", [R, 2, 2, D])
        st1 = sb("st1", [R, 2, 6]); mv1 = sb("mv1", [R, 2, 2]); ln1 = sb("ln1", [R, 2]); rs1 = sb("rs1", [R, 2])
        xn = sb("xn", [R, 2, D])
        xnT = sb("xnT", [P, KD, 2 * R])
        fgT = sb("fgT", [P, 2 * R])
        qsg = sb("qsg", [P, 2, 2 * KD * R])
        kT = sb("kT", [P, KD, 2 * R])
        qB = sb("qB", [P, KD, 4, 2 * R])
        nl = sb("nl", [R, 2, HM])
        nl_hi = sb("nl_hi", [P, 2, HM], F32R); nl_lo = sb("nl_lo", [P, 2, HM], F32R)
        sums = sb("sums", [P, 3 * R], F32R)
        sig = sb("sig", [R, 2, HM]); srow = sb("srow", [R, 2, HM])
        gab = sb("gab", [P, 2 * KD * R]); sg = sb("sg", [P, 2, 2 * KD * R])
        v = sb("v", [P, 2, 2, D])
        eD = sb("eD", [R, 2, 2, HM]); ek = sb("ek", [R, 3, HM])
        S = sb("S", [P, 3, HM])
        ST = sb("ST", [P, 2, 4, 3 * R])
        PT = sb("PT", [P, ROUNDS, 3, 4 * R]); AT = sb("AT", [P, ROUNDS, 3, 4 * R])
        masks = sb("masks", [R, 3, 4 * R])
        u = sb("u", [R, 2, HM]); mx = sb("mx", [R, 2 * H])
        Z = sb("Z", [R, 2 * H]); rZ = sb("rZ", [R, 2 * H])
        rz2 = sb("rz2", [R, 2 * H]); QE = sb("QE", [R, 2, HM]); QET = sb("QET", [P, 4, 2, 2 * R])
        ogn = sb("ogn", [P, KD, 2 * R])
        sq = sb("sq", [P, KD, 2 * R]); ss = sb("ss", [R, 4, 2 * H])
        scale = sb("scale", [R, 2, D])
        ogT = sb("ogT", [P, KD, 2 * R])
        rows = sb("rows", [R, 2, 2, COLS])
        st2 = sb("st2", [R, 2, 6]); mv2 = sb("mv2", [R, 2, 2]); ln2 = sb("ln2", [R, 2])
        xf = sb("xf", [R, 2, D]); xfT = sb("xfT", [P, KD, 2 * R])
        rt = sb("rt", [R, 8, 2 * E]); rsm = sb("rsm", [R, 4, 2])
        oh = sb("oh", [R, 2, E]); acc = sb("acc", [R, E]); acct = sb("acct", [R, E]); tokc = sb("tokc", [R, 2])
        slot = sb("slot", [R, 2, 2], U32)
        zero = sb("zero", [R, 16 // ZC * COLS])
        er = sb("er", [R, 2, 2, COLS]); res = sb("res", [R, 2, 2, COLS])
        xe = sb("xe", [R, 2, D]); xeT = sb("xeT", [P, KD, SLOTS])
        hid = PT[:, :, :, :].rearrange("p n a t -> p (n a t)")[:, 0:KF * SLOTS].rearrange("p (k t) -> p k t", k=KF)
        yeT = sb("yeT", [P, KD, SLOTS]); yo = sb("yo", [R, 2, 2, D])
        ix0 = sb("ix0", [R, 2, 2]); ix = sb("ix", [R, 2, 2], U32)

        def const(name, rows_=R):
            a, b = CONST[name]
            return cst[0:rows_, a:b]

        def landed(b, par, dmas=1):
            return 8 * dmas * (b - par) + 16 * dmas

        def wait_count(eng, s, count):
            if not isinstance(count, int) or count > 0:
                eng.wait_ge(s, count)

        def flat(x):
            return x.rearrange("p k t -> p (k t)")

        N_WTS = 9
        block = ctx.enter_context(nc.Block())

        @block.sync
        def _(sp):
            def load_text(b, par):
                wait_count(sp, sem["h_kept"], b - 1)
                t = txt[bass.ds(b, 1)].rearrange("o t d -> (o t) d")
                sp.dma_start(h[IMG:R, par, 0, :], t[0:R - IMG]).then_inc(sem["text_in"][par], 16)
                sp.dma_start(h[0:N - R, par, 1, :], t[R - IMG:TXT]).then_inc(sem["text_in"][par], 16)

            def store_h1(b, par):
                sp.wait_ge(sem["h1"], b + 1)
                o = out[bass.ds(b, 1)].rearrange("o t d -> (o t) d")
                sp.dma_start(o[0:R], rows[0:R, par, 0, 0:D]).then_inc(sem["h1_stored"][par], 16)
                sp.dma_start(o[R:N], rows[0:N - R, par, 1, 0:D]).then_inc(sem["h1_stored"][par], 16)
                sp.wait_ge(sem["h1_stored"][par], landed(b, par, 2))
                sp.sem_inc(sem["rows_stored"], 1)

            half = KP // 2
            sp.dma_start(tokw[:, 0:half, :], tok_w[:, 0:half]).then_inc(sem["emb_in"][0], 16)
            sp.dma_start(tokw[:, half:KP, :], tok_w[:, half:KP]).then_inc(sem["emb_in"][1], 16)
            sp.dma_start(cst[:, :], consts).then_inc(sem["const_in"], 16)
            sp.wait_ge(sem["zero_set"], 1)
            load_text(0, 0)
            for dst, src in ((wfg[:, :, :], wfg1), (wqs[:, :, :], wq), (wks[:, :, :], wk), (wf2s[0:DK, :], wf2),
                             (wvs[:, :, :], wv), (wg2s[DK:2 * DK, :], wg2), (wos[:, :, :], wo), (nw[:, :], norm_w),
                             (wrs[:, :, :], wr)):
                sp.dma_start(dst, src).then_inc(sem["wts_in"], 16)
            load_text(1, 1)
            for c in range(ZC):
                sp.dma_start(table.rearrange("(c r a) d -> c r (a d)", c=ZC, r=R)[c], zero[:, :]
                             ).then_inc(sem["table_clear"], 16)
            sp.wait_ge(sem["embT_ps"], 1)
            for e in range(2):
                sp.dma_start(w1s[:, e], w1[e]).then_inc(sem["w1_in"][e], 16)
                sp.dma_start(w2s[:, e], w2[e]).then_inc(sem["w2_in"][e], 16)
            sp.sem_inc(sem["rows_stored"], 1)
            with sp.Fori(1, B // 2) as pair:
                i = 2 * pair
                load_text(i, 0)
                store_h1(i - 2, 0)
                load_text(i + 1, 1)
                store_h1(i - 1, 1)
            store_h1(B - 2, 0)
            store_h1(B - 1, 1)

            def table_rows(e):
                t = table.rearrange("(e t r) d -> e r t d", e=E, t=2)[bass.ds(e, 1)]
                return t.rearrange("o r t d -> (o r) t d")

            def load_rows(e, par):
                wait_count(sp, sem["xe_rows"], e - 1)
                sp.dma_start(er[:, par], table_rows(e)).then_inc(sem["rows_in"][par], 16)

            def load_residual(e, par):
                wait_count(sp, sem["yout"], e - 1)
                sp.dma_start(res[:, par], table_rows(e)).then_inc(sem["res_in"][par], 16)

            def load_weights(e, par):
                sp.wait_ge(sem["hid_ps"], 4 * (e - 1))
                sp.dma_start(w1s[:, par], w1[bass.ds(e, 1)].rearrange("o p k f -> (o p) k f")
                             ).then_inc(sem["w1_in"][par], 16)
                sp.wait_ge(sem["ye_ps"], e - 1)
                sp.dma_start(w2s[:, par], w2[bass.ds(e, 1)].rearrange("o p k f -> (o p) k f")
                             ).then_inc(sem["w2_in"][par], 16)

            for par in range(2):
                sp.wait_ge(sem["table_io"][par], 16 * B)
            load_rows(0, 0)
            load_rows(1, 1)
            load_residual(0, 0)
            load_residual(1, 1)
            with sp.Fori(1, E // 2) as pair:
                e = 2 * pair
                load_rows(e, 0)
                load_weights(e, 0)
                load_residual(e, 0)
                load_rows(e + 1, 1)
                load_weights(e + 1, 1)
                load_residual(e + 1, 1)
            for par in range(2):
                sp.wait_ge(sem["out_rows"][par], 16 * E)
                sp.wait_ge(sem["h1_stored"][par], 16 * B)

        @block.tensor
        def _(pe):
            ident = const("ident", P)

            def mm(o, lhsT, rhs, start=True, stop=True):
                return nc.tensor.matmul(o, lhsT, rhs, start=start, stop=stop)

            def embed_all():
                for part in range(2):
                    pe.wait_ge(sem["emb_in"][part], 16 * (2 + part))
                    for c, k in ((c, k) for c in range(KD) for k in range(part * KP // 2, (part + 1) * KP // 2)):
                        x = mm(psF[:, c, 0:B * IMG], tokw[:, k, c * P:(c + 1) * P], xpat[:, k, :],
                               k == 0, k == KP - 1)
                x.then_inc(sem["embT_ps"], 1)

            def turn_embeddings():
                for b in range(B):
                    bank, at = [2, 3, 0, 1][b // 2], (b % 2) * D
                    for c in range(KD):
                        x = nc.tensor.transpose(psF[0:IMG, bank, at + c * P:at + (c + 1) * P],
                                                embT[:, c, b * IMG:(b + 1) * IMG], ident)
                    if b % 2:
                        x.then_inc(sem["emb_ps"], 1)

            def turn(o, src, done):
                for t in range(2):
                    for k in range(KD):
                        x = nc.tensor.transpose(o[:, k * 2 * R + t * R:k * 2 * R + (t + 1) * R],
                                                src[:, t, k * P:(k + 1) * P], const("ident")[:, 0:R])
                x.then_inc(done, 1)

            def turn_xn(b):
                pe.wait_ge(sem["xn"], b + 1)
                wait_count(pe, sem["ST"], b)
                turn(psF[:, 1, :], xn, sem["xnT_ps"])

            def project_fg_qk(b):
                pe.wait_ge(sem["xnT"], b + 1)
                for k in range(KD):
                    x = mm(psF[0:2 * DK, 0, 0:2 * R], wfg[:, k, :], xnT[:, k, :], k == 0, k == KD - 1)
                x.then_inc(sem["fg_ps"], 1)
                for w, bank in ((wqs, 2), (wks, 3)):
                    for c in range(KD):
                        for k in range(KD):
                            x = mm(psF[:, bank, c * 2 * R:(c + 1) * 2 * R], w[:, k, c * P:(c + 1) * P],
                                   xnT[:, k, :], k == 0, k == KD - 1)
                x.then_inc(sem["qk_ps"], 1)

            def forget_gates(b):
                pe.wait_ge(sem["fgT"], b + 1)
                for t in range(2):
                    x = mm(psF[0:R, t, :], fgT[:, t * R:(t + 1) * R], wf2s[:, :])
                x.then_inc(sem["f_ps"], 1)

            def values(b):
                pe.wait_ge(sem["qkT"], b + 1)
                for t in range(2):
                    for k in range(KD):
                        x = mm(psF[0:R, 2, t * D:(t + 1) * D], xnT[:, k, t * R:(t + 1) * R], wvs[:, k, :],
                               k == 0, k == KD - 1)
                x.then_inc(sem["v_ps"], 1)

            def gate(b):
                for c in range(KD):
                    x = mm(psF[:, 3, c * 2 * R:(c + 1) * 2 * R], wg2s[:, c * P:(c + 1) * P], fgT[:, :])
                x.then_inc(sem["g_ps"], 1)

            def decays(b):
                pe.wait_ge(sem["nl_hi"], b + 1)
                pe.wait_ge(sem["nl_lo"], b + 1)
                centre, cross0, cross1 = (sums[:, n * R:(n + 1) * R] for n in range(3))
                for t in range(2):
                    mm(psF[0:R, t, :], centre, nl_hi[:, t, :], True, False)
                    x = mm(psF[0:R, t, :], centre, nl_lo[:, t, :], False, True)
                x.then_inc(sem["d_ps"], 1)
                pe.wait_ge(sem["v"], b + 1)
                mm(psF[0:R, 2, :], cross0, nl_hi[:, 0, :], True, False)
                mm(psF[0:R, 2, :], cross0, nl_lo[:, 0, :], False, False)
                mm(psF[0:R, 2, :], cross1, nl_hi[:, 1, :], False, False)
                mm(psF[0:R, 2, :], cross1, nl_lo[:, 1, :], False, True).then_inc(sem["e_ps"], 1)

            def turn_slots(b, heads, route=False):
                for hp in heads:
                    if hp == 0:
                        pe.wait_ge(sem["S_rows"], b + 1)
                        pe.wait_ge(sem["eD"], b + 1)
                    if hp == 3:
                        pe.wait_ge(sem["g_exp"], b + 1)
                        if route:
                            pe.wait_ge(sem["slotx"], b - 1)
                    for a in range(3):
                        x = nc.tensor.transpose(psF[:, hp, a * R:(a + 1) * R], S[0:R, a, hp * P:(hp + 1) * P],
                                                const("ident")[:, 0:R])
                if heads[-1] == 3:
                    x.then_inc(sem["ST_ps"], 1)

            def qk_products(b, n):
                if n == 0:
                    wait_count(pe, sem["a_kept"], ROUNDS * b)
                    pe.wait_ge(sem["qkT"], b + 1)
                else:
                    pe.wait_ge(sem["p_kept"], ROUNDS * b + n)
                for pair in range(2):
                    mm(psB[0:R, pair, 0:4 * R], kT[:, n, 0:R],
                       qB[:, n, 2 * pair:2 * pair + 2, :].rearrange("p h t -> p (h t)"))
                mm(psB[0:R, 2, 0:4 * R].rearrange("r (h t) -> r h t", h=4), kT[:, n, R:2 * R],
                   qB[:, n, :, R:2 * R]).then_inc(sem["p_ps"], 1)

            def slot_scores(b):
                pe.wait_ge(sem["p_kept"], ROUNDS * (b + 1))
                pe.wait_ge(sem["S_rows"], b + 1)
                for hh in range(H):
                    m = slice(hh * M, (hh + 1) * M)
                    n, pair, two = hh // 4, hh % 4 // 2, hh % 2 * 2 * R
                    mm(psB[0:R, 0, m], PT[:, n, pair, two:two + R], S[:, 0, m])
                    mm(psB[0:R, 1, m], PT[:, n, pair, two + R:two + 2 * R], S[:, 1, m], True, False)
                    x = mm(psB[0:R, 1, m], PT[:, n, 2, hh % 4 * R:(hh % 4 + 1) * R], S[:, 2, m], False, True)
                x.then_inc(sem["o_ps"], 1)

            def turn_QE(b):
                pe.wait_ge(sem["QE"], b + 1)
                for hp in range(4):
                    for t in range(2):
                        at = (hp % 2) * 2 * R + t * R
                        x = nc.tensor.transpose(psB[:, 1 + hp // 2, at:at + R], QE[:, t, hp * P:(hp + 1) * P],
                                                const("ident")[:, 0:R])
                x.then_inc(sem["QET_ps"], 1)

            def slot_weights(b, par, n):
                if n == 0:
                    pe.wait_ge(sem["QETa"], b + 1)
                    pe.wait_ge(sem["QETb"], b + 1)
                    pe.wait_ge(sem["ST"], b + 1)
                else:
                    pe.wait_ge(sem["a_kept"], ROUNDS * b + n)
                for pair in range(2):
                    qe, st = QET[:, 2 * n + pair], ST[:, par, 2 * n + pair, :]
                    both = psB[:, pair, 0:4 * R].rearrange("p (h t) -> p h t", h=2)
                    last = psB[:, 2, 2 * pair * R:2 * (pair + 1) * R].rearrange("p (h t) -> p h t", h=2)
                    mm(both[0:R, :, R:2 * R], st[:, R:2 * R], qe[:, :, R:2 * R])
                    for o, k0, q0 in ((both, 0, 0), (last, 2 * R, R)):
                        mm(o[0:CUT, :, 0:CUT], st[:, k0:k0 + CUT], qe[:, :, q0:q0 + CUT])
                        x = mm(o[0:R, :, CUT:R], st[:, k0:k0 + R], qe[:, :, q0 + CUT:q0 + R])
                x.then_inc(sem["a_ps"], 1)

            def mix_values(b, par):
                wait_count(pe, sem["xfT"], b)
                for hh in range(H):
                    c, at = slice(hh * DK, (hh + 1) * DK), hh // 4 * 2 * R
                    ps = slice(hh % 4 * DK, (hh % 4 + 1) * DK)
                    n, pair, two = hh // 4, hh % 4 // 2, hh % 2 * 2 * R
                    if hh % 4 == 0:
                        pe.wait_ge(sem["a_kept"], ROUNDS * b + n + 1)
                    mm(psC[ps, at:at + 2 * R], v[:, par, 0, c], AT[:, n, pair, two:two + 2 * R], True, False)
                    x = mm(psC[ps, at + R:at + 2 * R], v[:, par, 1, c], AT[:, n, 2, hh % 4 * R:(hh % 4 + 1) * R],
                           False, True)
                x.then_inc(sem["ov_ps"], 1)

            def head_sums(b):
                pe.wait_ge(sem["sq"], b + 1)
                for t in range(2):
                    for k in range(KD):
                        at = t * H + k * 4
                        x = mm(psC[0:R, at:at + 4], sq[:, k, t * R:(t + 1) * R], const("heads", P))
                x.then_inc(sem["ss_ps"], 1)

            def turn_scale(b):
                pe.wait_ge(sem["scale"], b + 1)
                turn(psC, scale, sem["scale_ps"])

            def output_projection(b):
                pe.wait_ge(sem["ogT"], b + 1)
                for t in range(2):
                    for k in range(KD):
                        x = mm(psC[0:R, t * D:(t + 1) * D], ogT[:, k, t * R:(t + 1) * R], won[:, k, :],
                               k == 0, k == KD - 1)
                x.then_inc(sem["wo_ps"], 1)

            def turn_xf(b):
                pe.wait_ge(sem["xf"], b + 1)
                turn(psC, xf, sem["xfT_ps"])

            def logits(b, front):
                pe.wait_ge(sem["xfT"], b + 1)
                if front:
                    pe.wait_ge(sem["g_exp"], b + 3)
                for t in range(2):
                    for k in range(KD):
                        x = mm(lgs[:, t * E:(t + 1) * E], xfT[:, k, t * R:(t + 1) * R], wrs[:, k, :],
                               k == 0, k == KD - 1)
                x.then_inc(sem["lg_ps"], 1)

            def ranks(b):
                pe.wait_ge(sem["ohv"], b + 1)
                pe.wait_ge(sem["acc2"], b + 1)
                before, ones = const("before"), const("ones")
                r0, r1 = ranked[:, 0:E], ranked[:, E:2 * E]
                mm(r0, before, oh[:, 0, :], True, False)
                mm(r0, ones, acc[:, :], False, True)
                mm(r1, before, oh[:, 1, :], True, False)
                mm(r1, ones, oh[:, 0, :], False, False)
                mm(r1, ones, acc[:, :], False, True).then_inc(sem["rank_ps"], 1)

            def step(i, par, front=True, attend=True, route=True):
                b, bp, c = i - 1, 1 - par, i - 2
                if attend:
                    qk_products(b, 0)
                if front:
                    turn_xn(i)
                if route:
                    head_sums(c)
                if front:
                    project_fg_qk(i)
                if attend:
                    qk_products(b, 1)
                if front:
                    forget_gates(i)
                if route:
                    turn_scale(c)
                if attend:
                    slot_scores(b)
                if route:
                    output_projection(c)
                if front:
                    values(i)
                    decays(i)
                if attend:
                    turn_QE(b)
                if front:
                    gate(i)
                if attend:
                    slot_weights(b, bp, 0)
                if route:
                    turn_xf(c)
                if front:
                    turn_slots(i, range(3))
                if route:
                    logits(c, front)
                if attend:
                    slot_weights(b, bp, 1)
                if route:
                    ranks(c)
                if attend:
                    mix_values(b, bp)
                if front:
                    turn_slots(i, range(3, 4), route)

            embed_all()
            pe.wait_ge(sem["const_in"], 16)
            pe.wait_ge(sem["embT"], 1)
            turn_embeddings()
            pe.wait_ge(sem["img_kept"], 4)
            pe.wait_ge(sem["wts_in"], 16 * N_WTS)
            step(0, 0, attend=False, route=False)
            pe.wait_ge(sem["wo_scaled"], 1)
            step(1, 1, route=False)
            with pe.Fori(1, B // 2) as pair:
                i = 2 * pair
                step(i, 0)
                step(i + 1, 1)
            step(B, 0, front=False)
            step(B + 1, 1, front=False, attend=False)

            def turn_inputs(e):
                pe.wait_ge(sem["xe_rows"], e + 1)
                wait_count(pe, sem["xeT"], e)
                turn(psB[:, 0, :], xe, sem["xeT_ps"])

            def hidden(e, par):
                pe.wait_ge(sem["w1_in"][par], landed(e, par))
                pe.wait_ge(sem["xeT"], e + 1)
                for g in range(4):
                    wait_count(pe, sem["hid"], 4 * e + g - 3)
                    for f in range(2):
                        for k in range(KD):
                            c = (2 * g + f) * P
                            x = mm(psF[:, g, f * SLOTS:(f + 1) * SLOTS], w1s[:, par, k, c:c + P], xeT[:, k, :],
                                   k == 0, k == KD - 1)
                    x.then_inc(sem["hid_ps"], 1)

            def outputs(e, par):
                pe.wait_ge(sem["w2_in"][par], landed(e, par))
                pe.wait_ge(sem["hid"], 4 * (e + 1))
                wait_count(pe, sem["yeT"], e)
                for c in range(KD):
                    for k in range(KF):
                        x = mm(psB[:, 1, c * SLOTS:(c + 1) * SLOTS], w2s[:, par, k, c * P:(c + 1) * P], hid[:, k, :],
                               k == 0, k == KF - 1)
                x.then_inc(sem["ye_ps"], 1)

            def turn_outputs(e):
                pe.wait_ge(sem["yeT"], e + 1)
                for t in range(2):
                    for c in range(KD):
                        x = nc.tensor.transpose(psB[0:R, 2, t * D + c * P:t * D + (c + 1) * P],
                                                yeT[:, c, t * R:(t + 1) * R], ident)
                x.then_inc(sem["yb_ps"], 1)

            turn_inputs(0)
            hidden(0, 0)
            turn_inputs(1)
            outputs(0, 0)
            hidden(1, 1)
            with pe.Fori(1, E // 2) as pair:
                for par in range(2):
                    e = 2 * pair + par
                    turn_inputs(e)
                    turn_outputs(e - 2)
                    outputs(e - 1, 1 - par)
                    hidden(e, par)
            pe.wait_ge(sem["yout"], E - 2)
            turn_outputs(E - 2)
            outputs(E - 1, 1)
            pe.wait_ge(sem["yout"], E - 1)
            turn_outputs(E - 1)

        @block.scalar
        def _(act):
            half = KP // 2
            act.dma_start(xpat[:, 0:half, :], patches[:, 0:half]).then_inc(sem["emb_in"][0], 16)
            act.dma_start(xpat[:, half:KP, :], patches[:, half:KP]).then_inc(sem["emb_in"][1], 16)
            act.dma_start(bias[:, :], tok_b).then_inc(sem["emb_in"][1], 16)
            nc.scalar.preload_act_table_set("natural_log_exp_and_others")

            def fn(o, i, f, done, **kw):
                return nc.scalar.activation(o, i, f, **kw).then_inc(done, 1)

            def embedding_bias():
                act.wait_ge(sem["embT_ps"], 1)
                for c in range(KD):
                    x = nc.scalar.activation(embT[:, c, :], psF[:, c, 0:B * IMG], ACT.Identity, bias=bias[:, c:c + 1])
                x.then_inc(sem["embT"], 1)

            def keep_images():
                for n in range(B // 2):
                    act.wait_ge(sem["emb_ps"], n + 1)
                    fn(img[:, 2 * n:2 * n + 2, :].rearrange("r b d -> r (b d)"), psF[0:IMG, [2, 3, 0, 1][n], :], ACT.Copy,
                       sem["img_kept"])

            def place_image(b, par):
                act.wait_ge(sem["img_kept"], 1 if isinstance(b, int) and b < 2 else B // 2)
                wait_count(act, sem["h_kept"], b - 1)
                fn(h[0:IMG, par, 0, :], img[:, bass.ds(b, 1), :].rearrange("r o d -> r (o d)"), ACT.Copy, sem["h_img"])

            def rstd(b, mv, ln, o, ready, mid, done):
                act.wait_ge(ready, b + 1)
                fn(ln[:, :], mv[:, :, 1], ACT.Ln, mid, bias=const("lneps"))
                act.wait_ge(mid, b + 1)
                fn(o, ln[:, :], ACT.Exp, done, scale=-0.5)

            def head_squares(b):
                act.wait_ge(sem["ogn"], b + 1)
                fn(sq[:, :, :], ogn[:, :, :], ACT.Square, sem["sq"])

            def head_rms(b):
                act.wait_ge(sem["ss3"], b + 1)
                fn(ss[:, 2, :], ss[:, 1, :], ACT.Ln, sem["ss_ln"])
                act.wait_ge(sem["ss_ln"], b + 1)
                fn(ss[:, 3, :], ss[:, 2, :], ACT.Exp, sem["rms"], scale=-0.5)

            def keep(b, dst, src, ready, done):
                act.wait_ge(ready, b + 1)
                fn(dst, src, ACT.Copy, done)

            def sigmoid_qk(b):
                act.wait_ge(sem["qk_ps"], b + 1)
                wait_count(act, sem["qkT"], b)
                fn(qsg[:, :, :], psF[:, 2:4, 0:4 * R], ACT.Exp, sem["q_exp"], scale=-1.0)
                act.wait_ge(sem["q_exp"], b + 1)
                fn(qsg[:, :, :], qsg[:, :, :], ACT.Ln, sem["q_ln"], bias=1.0)
                act.wait_ge(sem["q_ln"], b + 1)
                fn(qsg[:, :, :], qsg[:, :, :], ACT.Exp, sem["q_sig"], scale=-1.0)

            def forget(b):
                act.wait_ge(sem["f_ps"], b + 1)
                wait_count(act, sem["nl_lo"], b)
                fn(nl[:, :, :], psF[0:R, 0:2, :], ACT.Exp, sem["f_exp"], scale=-1.0)
                act.wait_ge(sem["f_exp"], b + 1)
                fn(nl[:, :, :], nl[:, :, :], ACT.Ln, sem["f_ln"], bias=1.0)
                act.wait_ge(sem["f_ln"], b + 1)
                wait_count(act, sem["e_ps"], b)
                fn(nl_hi[0:R], nl[:, :, :], ACT.Copy, sem["nl_hi"])

            def gates(b):
                wait_count(act, sem["s"], b)
                fn(sig[:, :, :], nl[:, :, :], ACT.Exp, sem["f_sig"], scale=-1.0)

            def sigmoid_gate(b, par):
                act.wait_ge(sem["g_ps"], b + 1)
                fn(gab[:, :], psF[:, 3, 0:4 * R], ACT.Exp, sem["g_exp"], scale=-1.0)
                act.wait_ge(sem["g_exp"], b + 1)
                fn(gab[:, :], gab[:, :], ACT.Ln, sem["g_ln"], bias=1.0)
                act.wait_ge(sem["g_ln"], b + 1)
                wait_count(act, sem["ogn"], b - 1)
                fn(sg[:, par], gab[:, :], ACT.Exp, sem["g_sig"], scale=-1.0)

            def keep_v(b, par):
                wait_count(act, sem["ov_ps"], b - 1)
                keep(b, v[0:R, par].rearrange("r t d -> r (t d)"), psF[0:R, 2, :], sem["v_ps"], sem["v"])

            def decay_keys(b):
                act.wait_ge(sem["d_ps"], b + 1)
                wait_count(act, sem["S_rows"], b)
                fn(ek[:, 0::2, :], psF[0:R, 0:2, :], ACT.Exp, sem["ekD"])

            def decay_cross(b):
                act.wait_ge(sem["e_ps"], b + 1)
                fn(ek[:, 1, :], psF[0:R, 2, :], ACT.Exp, sem["ecD"], scale=-1.0)

            def decay_queries(b, par):
                wait_count(act, sem["QE"], b - 1)
                fn(eD[:, par], psF[0:R, 0:2, :], ACT.Exp, sem["eD"], scale=-1.0)

            def keep_QET(b):
                keep(b, QET[0:M, :, 0, :].rearrange("p (a c) t -> p a c t", a=2),
                     psB[0:M, 1:3, 0:4 * R].rearrange("p a (c t) -> p a c t", c=2), sem["QET_ps"], sem["QETa"])

            def keep_ST(b, par):
                keep(b, ST[:, par], psF[:, 0:4, 0:3 * R], sem["ST_ps"], sem["ST"])

            def numerators(b):
                act.wait_ge(sem["umx"], b + 1)
                fn(u[:, :, :], u[:, :, :], ACT.Exp, sem["pexp"])

            def logit_exps(b):
                act.wait_ge(sem["ldm"], b + 1)
                fn(rt[:, 1, :], rt[:, 0, :], ACT.Exp, sem["lexp"])

            def step(i, par, front=True, attend=True, route=True):
                b, bp, c = i - 1, 1 - par, i - 2
                if front:
                    place_image(i, par)
                if attend:
                    keep_ST(b, bp)
                if front:
                    rstd(i, mv1, ln1, rs1[:, :], sem["mv1"], sem["ln1"], sem["rstd1"])
                if route:
                    head_squares(c)
                if front:
                    keep(i, flat(xnT[:, :, :]), psF[:, 1, 0:4 * R], sem["xnT_ps"], sem["xnT"])
                if route:
                    head_rms(c)
                if front:
                    sigmoid_qk(i)
                    forget(i)
                    gates(i)
                    keep_v(i, par)
                if attend:
                    numerators(b)
                if front:
                    decay_keys(i)
                    decay_cross(i)
                if route:
                    rstd(c, mv2, ln2, rows[:, par, :, C_RSTD], sem["mv2"], sem["ln2"], sem["rstd2"])
                if attend:
                    keep_QET(b)
                if front:
                    decay_queries(i, par)
                    sigmoid_gate(i, par)
                if route:
                    keep(c, flat(xfT[:, :, :]), psC[:, 0:4 * R], sem["xfT_ps"], sem["xfT"])
                    logit_exps(c)

            act.wait_ge(sem["const_in"], 16)
            act.wait_ge(sem["emb_in"][1], 16 * 3)
            embedding_bias()
            keep_images()
            step(0, 0, attend=False, route=False)
            step(1, 1, route=False)
            with act.Fori(1, B // 2) as pair:
                i = 2 * pair
                step(i, 0)
                step(i + 1, 1)
            step(B, 0, front=False)
            step(B + 1, 1, front=False, attend=False)

            def keep_inputs(e):
                keep(e, flat(xeT[:, :, :]), psB[:, 0, 0:4 * R], sem["xeT_ps"], sem["xeT"])

            def keep_outputs(e):
                keep(e, flat(yeT[:, :, :]), psB[:, 1, 0:4 * R], sem["ye_ps"], sem["yeT"])

            def relu(e):
                for g in range(4):
                    act.wait_ge(sem["hid_ps"], 4 * e + g + 1)
                    fn(flat(hid[:, 2 * g:2 * g + 2, :]), psF[:, g, 0:4 * R], ACT.Relu, sem["hid"])

            keep_inputs(0)
            relu(0)
            keep_inputs(1)
            keep_outputs(0)
            relu(1)
            with act.Fori(1, E // 2) as pair:
                for par in range(2):
                    e = 2 * pair + par
                    keep_inputs(e)
                    act.wait_ge(sem["yb_ps"], e - 1)
                    keep_outputs(e - 1)
                    relu(e)
            act.wait_ge(sem["yb_ps"], E - 1)
            keep_outputs(E - 1)

        @block.vector
        def _(dve):
            def tt(o, a, b_, op, done):
                return nc.vector.tensor_tensor(o, a, b_, op).then_inc(done, 1)

            def apart():
                dve.wait_ge(sem["const_in"], 16)

            def hidden_stats(b, par):
                dve.wait_ge(sem["text_in"][par], landed(b, par, 2))
                dve.wait_ge(sem["h_img"], b + 1)
                for t in range(2):
                    x = nc.vector.bn_stats(st1[:, t, :], h[:, par, t, :])
                x.then_inc(sem["stats1"], 1)
                apart()
                dve.wait_ge(sem["stats1"], b + 1)
                for t in range(2):
                    x = nc.vector.bn_aggr(mv1[:, t, :], st1[:, t, :])
                x.then_inc(sem["mv1"], 1)

            def layernorm1(b, par):
                dve.wait_ge(sem["rstd1"], b + 1)
                wait_count(dve, sem["xnT_ps"], b)
                for t in range(2):
                    x = nc.vector.tensor_scalar(xn[:, t, :], h[:, par, t, :], mv1[:, t, 0:1], rs1[:, t:t + 1],
                                                ALU.subtract, ALU.mult)
                x.then_inc(sem["xn"], 1)

            def keep_fg(b):
                dve.wait_ge(sem["fg_ps"], b + 1)
                nc.vector.tensor_copy(fgT[0:2 * DK, :], psF[0:2 * DK, 0, 0:2 * R]).then_inc(sem["fgT"], 1)

            def silu_qk(b):
                dve.wait_ge(sem["q_sig"], b + 1)
                wait_count(dve, sem["p_ps"], ROUNDS * b)
                nc.vector.tensor_tensor(flat(kT[:, :, :]), psF[:, 3, 0:4 * R], qsg[:, 1, :], ALU.mult)
                for g in range(4):
                    ps = slice(g * DK, (g + 1) * DK)
                    x = nc.vector.tensor_tensor(qB[ps, :, g, :], psF[ps, 2, 0:4 * R].rearrange("p (k t) -> p k t", k=KD),
                                                qsg[ps, 0, :].rearrange("p (k t) -> p k t", k=KD), ALU.mult)
                x.then_inc(sem["qkT"], 1)

            def keep_QET(b):
                dve.wait_ge(sem["QET_ps"], b + 1)
                nc.vector.tensor_copy(QET[M:P, :, 1, :].rearrange("p (a c) t -> p a c t", a=2),
                                      psB[M:P, 1:3, 0:4 * R].rearrange("p a (c t) -> p a c t", c=2)
                                      ).then_inc(sem["QETb"], 1)

            def mask_P(b, n):
                dve.wait_ge(sem["p_ps"], ROUNDS * b + n + 1)
                tt(PT[0:R, n], psB[0:R, 0:3, 0:4 * R], masks[:, :, :], ALU.mult, sem["p_kept"])

            def mask_A(b, n):
                dve.wait_ge(sem["a_ps"], ROUNDS * b + n + 1)
                nc.vector.scalar_tensor_tensor(
                    out=AT[0:R, n], in0=psB[0:R, 0:3, 0:4 * R], scalar=ABIG,
                    in1=masks[:, :, :], op0=ALU.min, op1=ALU.mult).then_inc(sem["a_kept"], 1)

            def slots(x):
                return x[:, :, :].rearrange("r t (h m) -> r (t h) m", m=M)

            def softmax_shift(b, par):
                dve.wait_ge(sem["o_ps"], b + 1)
                tt(u[:, :, :], psB[0:R, 0:2, :], eD[:, par], ALU.mult, sem["u"])
                dve.wait_ge(sem["u"], b + 1)
                nc.vector.tensor_reduce(mx[:, :], slots(u), AX_X, ALU.max).then_inc(sem["umax"], 1)
                dve.wait_ge(sem["umax"], b + 1)
                tt(slots(u), slots(u), mx[:, :].unsqueeze(2).to_broadcast([R, 2 * H, M]), ALU.subtract, sem["umx"])

            def scale_queries(b, par):
                dve.wait_ge(sem["pexp"], b + 1)
                wait_count(dve, sem["QET_ps"], b)
                tt(QE[:, :, :], u[:, :, :], eD[:, par], ALU.mult, sem["QE"])

            def denominators(b):
                nc.vector.tensor_reduce(Z[:, :], slots(u), AX_X, ALU.add).then_inc(sem["Z"], 1)
                dve.wait_ge(sem["Z"], b + 1)
                nc.vector.reciprocal(rZ[:, :], Z[:, :]).then_inc(sem["rZ"], 1)
                dve.wait_ge(sem["rZ"], b + 1)
                tt(rz2[:, :], rZ[:, :], rZ[:, :], ALU.mult, sem["rz2"])

            def gate_output(b, par):
                dve.wait_ge(sem["ov_ps"], b + 1)
                dve.wait_ge(sem["g_sig"], b + 1)
                tt(flat(ogn[:, :, :]), psC[:, 0:4 * R], sg[:, par], ALU.mult, sem["ogn"])

            def scale_output(b):
                dve.wait_ge(sem["scale_ps"], b + 1)
                tt(flat(ogT[:, :, :]), psC[:, 0:4 * R], flat(ogn[:, :, :]), ALU.mult, sem["ogT"])

            def head_means(b):
                dve.wait_ge(sem["ss_ps"], b + 1)
                dve.wait_ge(sem["rz2"], b + 1)
                tt(ss[:, 0, :], psC[0:R, 0:2 * H], rz2[:, :], ALU.mult, sem["ss2"])
                dve.wait_ge(sem["ss2"], b + 1)
                nc.vector.tensor_scalar(ss[:, 1, :], ss[:, 0, :], 1.0 / DK, RMS_EPS, ALU.mult, ALU.add
                                        ).then_inc(sem["ss3"], 1)

            def residual_stats(b, par):
                dve.wait_ge(sem["wo_ps"], b + 1)
                dve.wait_ge(sem["h_kept"], b + 1)
                tt(rows[:, par, :, 0:D], psC[0:R, :].rearrange("r (t d) -> r t d", t=2), rows[:, par, :, 0:D],
                   ALU.add, sem["h1"])
                dve.wait_ge(sem["h1"], b + 1)
                for t in range(2):
                    x = nc.vector.bn_stats(st2[:, t, :], rows[:, par, t, 0:D])
                x.then_inc(sem["stats2"], 1)

            def residual_mean(b):
                apart()
                dve.wait_ge(sem["stats2"], b + 1)
                for t in range(2):
                    x = nc.vector.bn_aggr(mv2[:, t, :], st2[:, t, :])
                x.then_inc(sem["mv2"], 1)

            def layernorm2(b, par):
                dve.wait_ge(sem["rstd2"], b + 1)
                nc.vector.scalar_tensor_tensor(out=rows[:, par, :, C_NMR], in0=mv2[:, :, 0], scalar=-1.0,
                                               in1=rows[:, par, :, C_RSTD], op0=ALU.mult, op1=ALU.mult
                                               ).then_inc(sem["nmr"], 1)
                dve.wait_ge(sem["nmr"], b + 1)
                for t in range(2):
                    x = nc.vector.tensor_scalar(xf[:, t, :], rows[:, par, t, 0:D], rows[:, par, t, C_RSTD:C_RSTD + 1],
                                                rows[:, par, t, C_NMR:C_NMR + 1], ALU.mult, ALU.add)
                x.then_inc(sem["xf"], 1)

            def e3(x):
                return x.rearrange("r (t e) -> r t e", e=E)

            def choose_expert(b, par):
                def bc(x):
                    return x.unsqueeze(2).to_broadcast([R, 2, E])
                dve.wait_ge(sem["lg_ps"], b + 1)
                nc.vector.tensor_reduce(rsm[:, 0, :], e3(lgs), AX_X, ALU.max
                                        ).then_inc(sem["lmax"], 1)
                dve.wait_ge(sem["lmax"], b + 1)
                tt(e3(rt[:, 0, :]), e3(lgs), bc(rsm[:, 0, :]), ALU.subtract, sem["ldm"])
                dve.wait_ge(sem["ldm"], b + 1)
                nc.vector.scalar_tensor_tensor(out=rt[:, 2, :], in0=rt[:, 0, :], scalar=0.0, in1=const("rev"),
                                               op0=ALU.is_ge, op1=ALU.mult).then_inc(sem["pick"], 1)
                dve.wait_ge(sem["pick"], b + 1)
                nc.vector.tensor_reduce(rsm[:, 1, :], e3(rt[:, 2, :]), AX_X, ALU.max).then_inc(sem["pickmax"], 1)
                dve.wait_ge(sem["pickmax"], b + 1)
                tt(e3(rt[:, 3, :]), e3(const("rev")), bc(rsm[:, 1, :]), ALU.is_equal, sem["oh"])
                dve.wait_ge(sem["oh"], b + 1)
                dve.wait_ge(sem["acc2"], b + 1)
                tt(oh[:, :, :], e3(rt[:, 3, :]), e3(const("validE")), ALU.mult, sem["ohv"])

            def probability(b, par):
                dve.wait_ge(sem["lexp"], b + 1)
                nc.vector.tensor_reduce(rsm[:, 2, :], e3(rt[:, 1, :]), AX_X, ALU.add).then_inc(sem["lsum"], 1)
                dve.wait_ge(sem["lsum"], b + 1)
                nc.vector.reciprocal(rows[:, par, :, C_PROB], rsm[:, 2, :]).then_inc(sem["prob"], 1)

            def choose_slot(b, par):
                dve.wait_ge(sem["rank_ps"], b + 1)
                rank = ranked
                tt(rt[:, 4, :], rank, const("full"), ALU.is_ge, sem["over"])
                dve.wait_ge(sem["over"], b + 1)
                nc.vector.scalar_tensor_tensor(out=rt[:, 6, :], in0=rt[:, 4, :], scalar=FAR, in1=rank,
                                               op0=ALU.mult, op1=ALU.add).then_inc(sem["slotx"], 1)
                dve.wait_ge(sem["slotx"], b + 1)
                dve.wait_ge(sem["ohv"], b + 1)
                tt(rt[:, 7, :], rt[:, 6, :], oh[:, :, :].rearrange("r t e -> r (t e)"), ALU.mult, sem["slotoh"])
                tt(acct[:, :], oh[:, 0, :], oh[:, 1, :], ALU.add, sem["acc1"])
                dve.wait_ge(sem["slotoh"], b + 1)
                nc.vector.tensor_reduce(rsm[:, 3, :], e3(rt[:, 7, :]), AX_X, ALU.add).then_inc(sem["slotsum"], 1)
                dve.wait_ge(sem["acc1"], b + 1)
                tt(acc[:, :], acc[:, :], acct[:, :], ALU.add, sem["acc2"])
                dve.wait_ge(sem["slotsum"], b + 1)
                tt(slot[:, par, :], rsm[:, 3, :], const("far"), ALU.add, sem["slot"])

            def step(i, par, front=True, attend=True, route=True):
                b, bp, c = i - 1, 1 - par, i - 2
                if front:
                    hidden_stats(i, par)
                if route:
                    gate_output(c, par)
                if front:
                    layernorm1(i, par)
                if route:
                    denominators(c)
                if attend:
                    mask_P(b, 0)
                if route:
                    head_means(c)
                if front:
                    keep_fg(i)
                if attend:
                    mask_P(b, 1)
                if front:
                    silu_qk(i)
                if route:
                    scale_output(c)
                if attend:
                    softmax_shift(b, bp)
                if route:
                    residual_stats(c, par)
                if attend:
                    scale_queries(b, bp)
                if route:
                    residual_mean(c)
                if attend:
                    keep_QET(b)
                if route:
                    layernorm2(c, par)
                if attend:
                    mask_A(b, 0)
                if route:
                    choose_expert(c, par)
                    probability(c, par)
                if attend:
                    mask_A(b, 1)
                if route:
                    choose_slot(c, par)

            nc.vector.memset(h[64:R, :, 1, :], 0.0)
            for x in (wf2s[:, :], wg2s[:, :], fgT[2 * DK:P, :], qB[:, :, :, :], v[64:P],
                      S[64:P, :, :], PT[64:P], AT[64:P], QET[:, :, :, :]):
                nc.vector.memset(x, 0.0)
            nc.vector.memset(zero[:, :], 0.0).then_inc(sem["zero_set"], 1)
            dve.wait_ge(sem["const_in"], 16)
            nc.vector.tensor_copy(sums[:, :], cst[:, CONST["centre"][0]:CONST["cross1"][1]])
            for x in (nl_hi, nl_lo):
                nc.vector.tensor_copy(x[64:P].rearrange("p t m -> p (t m)"),
                                      cst[64:P, CONST["zero"][0]:CONST["zero"][0] + 1].to_broadcast([P - 64, 2 * HM]))
            tri, causal = const("mask")[:, 0:R], const("mask")
            for bank in range(2):
                nc.vector.tensor_copy(masks[:, bank, :].rearrange("r (h t) -> r h t", h=2),
                                      causal.unsqueeze(1).to_broadcast([R, 2, 2 * R]))
            nc.vector.tensor_copy(masks[:, 2, :].rearrange("r (h t) -> r h t", h=4),
                                  tri.unsqueeze(1).to_broadcast([R, 4, R]))
            nc.vector.tensor_copy(acc[:, :], const("first")).then_inc(sem["acc2"], 1)
            nc.vector.tensor_copy(tokc[:, :], const("tok")).then_inc(sem["zero_set"], 1)
            dve.wait_ge(sem["zero_set"], 2)
            step(0, 0, attend=False, route=False)
            dve.wait_ge(sem["wts_in"], 16 * N_WTS)
            for k in range(KD):
                x = nc.vector.tensor_scalar(won[:, k, :], wos[:, k, :], nw[:, k:k + 1], None, ALU.mult)
            x.then_inc(sem["wo_scaled"], 1)
            step(1, 1, route=False)
            with dve.Fori(1, B // 2) as pair:
                i = 2 * pair
                step(i, 0)
                step(i + 1, 1)
            step(B, 0, front=False)
            step(B + 1, 1, front=False, attend=False)

            def expert_inputs(e, par):
                dve.wait_ge(sem["rows_in"][par], landed(e, par))
                wait_count(dve, sem["xeT_ps"], e)
                for t in range(2):
                    x = nc.vector.tensor_scalar(xe[:, t, :], er[:, par, t, 0:D], er[:, par, t, C_RSTD:C_RSTD + 1],
                                                er[:, par, t, C_NMR:C_NMR + 1], ALU.mult, ALU.add)
                x.then_inc(sem["xe_rows"], 1)

            def expert_outputs(e, par):
                dve.wait_ge(sem["res_in"][par], landed(e, par))
                dve.wait_ge(sem["out_free"], e + 1)
                nc.vector.tensor_scalar(ix0[:, par, :], res[:, par, :, C_TOK], 0.0, FAR + 1.0, ALU.is_equal, ALU.mult
                                        ).then_inc(sem["idx0"], 1)
                dve.wait_ge(sem["idx0"], e + 1)
                nc.vector.scalar_tensor_tensor(out=ix[:, par, :], in0=res[:, par, :, C_TOK], scalar=-1.0,
                                               in1=ix0[:, par, :], op0=ALU.add, op1=ALU.add).then_inc(sem["idx"], 1)
                dve.wait_ge(sem["yb_ps"], e + 1)
                for t in range(2):
                    x = nc.vector.scalar_tensor_tensor(out=yo[:, par, t, :], in0=psB[0:R, 2, t * D:(t + 1) * D],
                                                       scalar=res[:, par, t, C_PROB:C_PROB + 1],
                                                       in1=res[:, par, t, 0:D], op0=ALU.mult, op1=ALU.add)
                x.then_inc(sem["yout"], 1)

            expert_inputs(0, 0)
            expert_inputs(1, 1)
            with dve.Fori(1, E // 2) as pair:
                for par in range(2):
                    expert_inputs(2 * pair + par, par)
                    expert_outputs(2 * pair + par - 2, par)
            expert_outputs(E - 2, 0)
            expert_outputs(E - 1, 1)

        @block.gpsimd
        def _(pool):
            def keep_h(b, par):
                pool.wait_ge(sem["h_img"], b + 1)
                pool.wait_ge(sem["text_in"][par], landed(b, par, 2))
                wait_count(pool, sem["rows_stored"], b)
                nc.gpsimd.tensor_tensor(rows[:, par, :, 0:D], h[:, par],
                                        const("zero").unsqueeze(1).to_broadcast([R, 2, D]), ALU.add
                                        ).then_inc(sem["h_kept"], 1)
                nc.gpsimd.tensor_tensor(rows[:, par, :, C_TOK], tokc[:, :], const("zero")[:, 0:2], ALU.add
                                        ).then_inc(sem["tokset"], 1)
                pool.wait_ge(sem["tokset"], b + 1)
                nc.gpsimd.tensor_tensor(tokc[:, :], tokc[:, :], const("rowlen"), ALU.add).then_inc(sem["toknext"], 1)

            def low_part(b):
                pool.wait_ge(sem["nl_hi"], b + 1)
                wait_count(pool, sem["e_ps"], b)
                nc.gpsimd.tensor_tensor(nl_lo[0:R], nl[:, :, :], nl_hi[0:R].bitcast(F32), ALU.subtract
                                        ).then_inc(sem["nl_lo"], 1)

            def slot_values(b):
                pool.wait_ge(sem["f_sig"], b + 1)
                nc.gpsimd.tensor_tensor(srow[:, :, :], const("ones")[:, 0:1].unsqueeze(1).to_broadcast([R, 2, HM]),
                                        sig[:, :, :], ALU.subtract).then_inc(sem["s"], 1)

            def scale_slots(b):
                pool.wait_ge(sem["ekD"], b + 1)
                pool.wait_ge(sem["s"], b + 1)
                wait_count(pool, sem["o_ps"], b)
                wait_count(pool, sem["ST_ps"], b)
                nc.gpsimd.tensor_tensor(S[0:R, 0::2, :], srow[:, :, :], ek[:, 0::2, :], ALU.mult)
                pool.wait_ge(sem["ecD"], b + 1)
                nc.gpsimd.tensor_tensor(S[0:R, 1, :], srow[:, 0, :], ek[:, 1, :], ALU.mult
                                        ).then_inc(sem["S_rows"], 1)

            def normalise(b):
                pool.wait_ge(sem["rms"], b + 1)
                pool.wait_ge(sem["rZ"], b + 1)
                nc.gpsimd.tensor_tensor(scale[:, :, :].rearrange("r t (h c) -> r (t h) c", c=DK),
                                        ss[:, 3, :].unsqueeze(2).to_broadcast([R, 2 * H, DK]),
                                        rZ[:, :].unsqueeze(2).to_broadcast([R, 2 * H, DK]), ALU.mult
                                        ).then_inc(sem["scale"], 1)

            def dispatch(b, par):
                pool.wait_ge(sem["slot"], b + 1)
                pool.wait_ge(sem["prob"], b + 1)
                pool.wait_ge(sem["tokset"], b + 1)
                pool.sem_inc(sem["go_dispatch"], 1)
                for t in range(2):
                    nc.gpsimd.indirect_dma_start(
                        out=table, out_offset=bass.IndirectOffsetOnAxis(ap=slot[:, par, t:t + 1], axis=0),
                        in_=rows[:, par, t, :], in_offset=None, bounds_check=E * SLOTS - 1, oob_is_err=False
                        ).then_inc(sem["table_io"][par], 16)

            def step(i, par, front=True, attend=True, route=True):
                b, bp, c = i - 1, 1 - par, i - 2
                if route:
                    normalise(c)
                if attend:
                    keep_h(b, bp)
                if front:
                    low_part(i)
                    slot_values(i)
                    scale_slots(i)
                if route:
                    dispatch(c, par)
                    pool.wait_ge(sem["table_io"][par], landed(c, par, 2))

            pool.wait_ge(sem["const_in"], 16)
            pool.wait_ge(sem["zero_set"], 2)
            step(0, 0, attend=False, route=False)
            step(1, 1, route=False)
            pool.wait_ge(sem["table_clear"], 16 * ZC)
            with pool.Fori(1, B // 2) as pair:
                i = 2 * pair
                step(i, 0)
                step(i + 1, 1)
            step(B, 0, front=False)
            step(B + 1, 1, front=False, attend=False)

            out_rows = out.rearrange("b n d -> (b n) d")

            def scatter(e, par):
                pool.wait_ge(sem["yout"], e + 1)
                pool.wait_ge(sem["idx"], e + 1)
                pool.sem_inc(sem["go_scatter"], 1)
                for t in range(2):
                    nc.gpsimd.indirect_dma_start(
                        out=out_rows, out_offset=bass.IndirectOffsetOnAxis(ap=ix[:, par, t:t + 1], axis=0),
                        in_=yo[:, par, t, :], in_offset=None, bounds_check=B * N - 1, oob_is_err=False
                        ).then_inc(sem["out_rows"][par], 16)
                if not isinstance(e, int) or e > 0:
                    pool.wait_ge(sem["out_rows"][1 - par], landed(e - 1, 1 - par, 2))
                    pool.sem_inc(sem["out_free"], 1)

            pool.sem_inc(sem["out_free"], 2)
            for par in range(2):
                pool.wait_ge(sem["h1_stored"][par], 16 * B)
            scatter(0, 0)
            scatter(1, 1)
            with pool.Fori(1, E // 2) as pair:
                scatter(2 * pair, 0)
                scatter(2 * pair + 1, 1)


def shape_constants():
    c = np.zeros((P, CONST_COLS), np.float32)

    def put(name, a):
        lo, hi = CONST[name]
        c[:a.shape[0], lo:hi] = a

    i, t = np.arange(R)[:, None], np.arange(R)[None, :]
    tri = (i <= t)
    put("ident", np.eye(P))
    put("mask", np.concatenate([tri, np.ones((R, R))], 1))
    put("centre", (i <= t).astype(np.float32) - (i <= MID))
    put("cross0", i > t)
    put("cross1", np.broadcast_to(i <= MID, (R, R)))
    put("before", i < t)
    put("ones", np.ones((R, R)))
    put("rev", np.tile(E - np.arange(E), (R, 2)))
    put("full", np.tile(SLOTS * np.arange(E) + CAP, (R, 2)))
    put("first", SLOTS * np.arange(E)[None, :])
    real = np.ones((R, 2)); real[R - 1, 1] = 0
    put("validE", np.repeat(real, E, axis=1))
    put("far", (1 - real) * FAR)
    put("tok", np.arange(R)[:, None] + np.array([[1, R + 1]]))
    put("lneps", np.full((R, 1), LN_EPS))
    put("rowlen", np.full((R, 2), N))
    put("heads", np.repeat(np.eye(4), DK, axis=0))
    return c


def kernel(**inputs):
    import concourse.bacc as bacc
    from concourse.bass_utils import run_bass_kernel_spmd

    a = {k: np.asarray(x) for k, x in inputs.items()}

    def tiles(w):
        return w.reshape(-1, P, w.shape[-1]).transpose(1, 0, 2)

    patches = a["x"].reshape(B, 3, 7, PATCH, 7, PATCH).transpose(0, 2, 4, 1, 3, 5).reshape(B, IMG, KP, P)
    laid = {
        "patches": patches.transpose(3, 2, 0, 1).reshape(P, KP, B * IMG),
        "txt": a["txt"],
        "tok_w": tiles(a["L0_tok_W"].T),
        "tok_b": a["L0_tok_b"].reshape(KD, P).T,
        "wq": tiles(a["L0_attn_Wq"]), "wk": tiles(a["L0_attn_Wk"]), "wv": tiles(a["L0_attn_Wv"]),
        "wfg1": tiles(np.concatenate([a["L0_attn_Wf1"], a["L0_attn_Wg1"]], 1)),
        "wf2": a["L0_attn_Wf2"], "wg2": a["L0_attn_Wg2"], "wo": tiles(a["L0_attn_Wo"]),
        "norm_w": a["L0_attn_norm_w"].reshape(KD, P).T,
        "wr": tiles(a["L0_ffn_Wr"]),
        "w1": a["L0_ffn_W1"].reshape(E, KD, P, F).transpose(0, 2, 1, 3),
        "w2": a["L0_ffn_W2"].reshape(E, KF, P, D).transpose(0, 2, 1, 3),
        "consts": shape_constants(),
    }
    nc = bacc.Bacc("TRN2", target_bir_lowering=False, num_devices=1)
    arrays, args = {}, []
    for name, x in laid.items():
        x = np.ascontiguousarray(x)
        arrays["in_" + name] = x
        args.append(nc.dram_tensor("in_" + name, x.shape, mybir.dt.from_np(x.dtype), kind="ExternalInput").ap())
    args.append(nc.dram_tensor("out", (B, N, D), F32, kind="ExternalOutput").ap())
    program(nc, *args)
    r = run_bass_kernel_spmd(nc, [arrays], core_ids=[0])
    return r.results[0]["out"]
```
